# Optimizing a Trainium2 kernel written in Bass

```python
import numpy as np
import jax
import jax.numpy as jnp

def _softmax(x, axis=-1):
    return jax.nn.softmax(x, axis=axis)

def _gelu(x):
    return jax.nn.gelu(x, approximate=True)

def _silu(x):
    return jax.nn.silu(x)

def _sigmoid(x):
    return jax.nn.sigmoid(x)

def _layernorm(x, axis=-1, eps=1e-05):
    m = jnp.mean(x, axis=axis, keepdims=True)
    v = jnp.var(x, axis=axis, keepdims=True)
    return (x - m) / jnp.sqrt(v + eps)

def _scatter_add(tgt, idx, src, axis=0):
    return tgt.at[idx].add(src)

def _segment_sum(src, seg, n):
    return jax.ops.segment_sum(src, seg, n)
kernel_name = 'mk_macaron_d1_jaxref_r4_919c31'

def setup_inputs(seed: int=0):
    np.random.seed(seed)
    _w = jnp.asarray

    def _L0_attn_setup():
        import jax, jax.numpy as jnp
        import numpy as np
        THETA = 10000.0

        def _rope(x, cos, sin):
            xr = x.reshape(*x.shape[:-1], -1, 2)
            x0, x1 = (xr[..., 0], xr[..., 1])
            o0 = x0 * cos - x1 * sin
            o1 = x0 * sin + x1 * cos
            return jnp.stack([o0, o1], axis=-1).reshape(x.shape)
        key = jax.random.key(seed)
        ks = jax.random.split(key, 7)
        B, S, D = (4, 512, 256)
        sd = 1.0 / np.sqrt(D)
        return {'x': jax.random.normal(ks[0], (B, S, D), dtype=jnp.float32), 'wq_w': jax.random.normal(ks[1], (D, D), dtype=jnp.float32) * sd, 'wq_b': jax.random.normal(ks[2], (D,), dtype=jnp.float32) * 0.01, 'wk_w': jax.random.normal(ks[3], (D, D), dtype=jnp.float32) * sd, 'wk_b': jax.random.normal(ks[4], (D,), dtype=jnp.float32) * 0.01, 'wv_w': jax.random.normal(ks[5], (D, D), dtype=jnp.float32) * sd, 'wv_b': jax.random.normal(ks[6], (D,), dtype=jnp.float32) * 0.01}
    _L0_attn_in = _L0_attn_setup()

    def _L0_ffn_setup():
        import jax, jax.numpy as jnp
        import numpy as np
        DIM = 256
        HIDDEN = 768
        SCALE = 1.0 / 127.0

        def _dequant(w_int, dtype):
            return w_int.astype(dtype) * jnp.asarray(SCALE, dtype)
        key = jax.random.key(seed)
        k_x, k_g, k_u, k_d = jax.random.split(key, 4)
        x = jax.random.normal(k_x, (4, 512, DIM), dtype=jnp.float32)
        w_gate = jax.random.randint(k_g, (HIDDEN, DIM), -127, 128, dtype=jnp.int32)
        w_up = jax.random.randint(k_u, (HIDDEN, DIM), -127, 128, dtype=jnp.int32)
        w_down = jax.random.randint(k_d, (DIM, HIDDEN), -127, 128, dtype=jnp.int32)
        return {'x': x, 'w_gate': w_gate, 'w_up': w_up, 'w_down': w_down}
    _L0_ffn_in = _L0_ffn_setup()
    _d = {'L0_attn_x': _L0_attn_in['x'], 'L0_attn_wq_w': _L0_attn_in['wq_w'], 'L0_attn_wq_b': _L0_attn_in['wq_b'], 'L0_attn_wk_w': _L0_attn_in['wk_w'], 'L0_attn_wk_b': _L0_attn_in['wk_b'], 'L0_attn_wv_w': _L0_attn_in['wv_w'], 'L0_attn_wv_b': _L0_attn_in['wv_b'], 'L0_ffn_w_gate': _L0_ffn_in['w_gate'], 'L0_ffn_w_up': _L0_ffn_in['w_up'], 'L0_ffn_w_down': _L0_ffn_in['w_down']}
    _x0 = _d['L0_attn_x']
    _d['L0_attn_x'] = jax.random.normal(jax.random.fold_in(jax.random.key(seed), 1), (16, 512, 256), dtype=_x0.dtype)
    del _x0
    return _d

def reference(L0_attn_x, L0_attn_wq_w, L0_attn_wq_b, L0_attn_wk_w, L0_attn_wk_b, L0_attn_wv_w, L0_attn_wv_b, L0_ffn_w_gate, L0_ffn_w_up, L0_ffn_w_down):

    def _L0_attn_ref(x, wq_w, wq_b, wk_w, wk_b, wv_w, wv_b):
        import jax, jax.numpy as jnp
        import numpy as np
        THETA = 10000.0

        def _rope(x, cos, sin):
            xr = x.reshape(*x.shape[:-1], -1, 2)
            x0, x1 = (xr[..., 0], xr[..., 1])
            o0 = x0 * cos - x1 * sin
            o1 = x0 * sin + x1 * cos
            return jnp.stack([o0, o1], axis=-1).reshape(x.shape)
        B, S, D = x.shape
        q = jnp.einsum('bsd,ed->bse', x, wq_w) + wq_b
        k = jnp.einsum('bsd,ed->bse', x, wk_w) + wk_b
        v = jnp.einsum('bsd,ed->bse', x, wv_w) + wv_b
        inv_freq = 1.0 / THETA ** (jnp.arange(0, D, 2, dtype=jnp.float32) / D)
        ang = jnp.arange(S, dtype=jnp.float32)[:, None] * inv_freq[None, :]
        cos, sin = (jnp.cos(ang), jnp.sin(ang))
        q = _rope(q, cos, sin)
        k = _rope(k, cos, sin)
        scores = jnp.einsum('bqd,bkd->bqk', q, k) / jnp.sqrt(jnp.float32(D))
        probs = jax.nn.softmax(scores.astype(jnp.float32), axis=-1)
        return jnp.einsum('bqk,bkd->bqd', probs, v)

    def _L0_ffn_ref(x, w_gate, w_up, w_down):
        import jax, jax.numpy as jnp
        import numpy as np
        DIM = 256
        HIDDEN = 768
        SCALE = 1.0 / 127.0

        def _dequant(w_int, dtype):
            return w_int.astype(dtype) * jnp.asarray(SCALE, dtype)
        wg = _dequant(w_gate, x.dtype)
        wu = _dequant(w_up, x.dtype)
        wd = _dequant(w_down, x.dtype)
        gate = jnp.einsum('bsd,hd->bsh', x, wg)
        up = jnp.einsum('bsd,hd->bsh', x, wu)
        h = jax.nn.silu(gate) * up
        return jnp.einsum('bsh,dh->bsd', h, wd)
    x = L0_attn_x
    x = x + 0.5 * _L0_ffn_ref(_layernorm(x, axis=-1), L0_ffn_w_gate, L0_ffn_w_up, L0_ffn_w_down)
    x = x + _L0_attn_ref(_layernorm(x, axis=-1), L0_attn_wq_w, L0_attn_wq_b, L0_attn_wk_w, L0_attn_wk_b, L0_attn_wv_w, L0_attn_wv_b)
    x = x + 0.5 * _L0_ffn_ref(_layernorm(x, axis=-1), L0_ffn_w_gate, L0_ffn_w_up, L0_ffn_w_down)
    return x

_drawn_inputs = setup_inputs


def setup_inputs(seed=0):
    import zlib

    import numpy as np

    out = dict(_drawn_inputs(seed))
    spreads = {}
    factors = {'L0_attn_wq_w': 22.76,
     'L0_attn_wq_b': 200.0,
     'L0_attn_wk_w': 22.744,
     'L0_attn_wk_b': 200.0,
     'L0_attn_wv_w': 22.726,
     'L0_attn_wv_b': 200.0}
    for name, (base, spread) in spreads.items():
        noise = np.random.default_rng([zlib.crc32(name.encode()), seed]).standard_normal(out[name].shape)
        drawn = base * np.exp(spread * noise) if base else spread * noise
        out[name] = jnp.asarray(drawn.astype(out[name].dtype))
    for name, factor in factors.items():
        out[name] = (out[name] * factor).astype(out[name].dtype)
    return out
```

```python
from contextlib import ExitStack

import numpy as np

import concourse.bass as bass
from concourse import mybir

F32 = mybir.dt.float32
F32R = mybir.dt.float32r
I32 = mybir.dt.int32
ALU = mybir.AluOpType
ACT = mybir.ActivationFunctionType
AX_X = mybir.AxisListType.X

P = 128
BATCHES, TOKENS, D = 16, 512, 256
HIDDEN = 768
TILES = TOKENS // P
DC = D // P
CHUNKS = HIDDEN // P
SLOTS = 2 * CHUNKS
EPS = 1e-5
THETA = 10000.0
WEIGHT_SCALE = 1.0 / 127.0
GATE, UP, DOWN = range(3)
Q, K, V = range(3)

FIRST, ATTEND, SECOND, SECOND_DOWN, AHEAD = "first", "attend", "second", "second_down", "ahead"
LAG = {AHEAD: -1, FIRST: 0, ATTEND: 1, SECOND: 2, SECOND_DOWN: 3}
START, STEADY, STEADY_END, END = -1, 4, 15, BATCHES + 3

ORDER = {
    "chunk": [(s, FIRST if s < CHUNKS else SECOND) for s in range(SLOTS)],
    "norm": [("n3a", SECOND), ("n3b", SECOND), ("n1a", AHEAD), ("n1b", AHEAD), ("n2a", FIRST), ("n2b", FIRST)],
    "turn": [("n2b", ATTEND), ("n3a", SECOND), ("n3b", SECOND), ("n1a", AHEAD), ("p0", ATTEND),
             ("p1", ATTEND), ("n1b", AHEAD), ("p2", ATTEND), ("p3", ATTEND), ("n2a", FIRST)],
    "out": [(f"second{t}", SECOND_DOWN) for t in range(TILES)]
    + [(name, stage) for t in range(TILES) for name, stage in ((f"attend{t}", ATTEND), (f"first{t}", FIRST))],
}


NORM_SLOT = {"n3a": 0, "n3b": 2, "n1a": 4, "n1b": 6, "n2a": 8, "n2b": 10}


def active(stage, i):
    return 0 <= i - LAG[stage] < BATCHES


class Step:

    def __init__(self, i, r=None):
        self.i, self.r = i, r

    def has(self, stage):
        return active(stage, self.i)

    def start(self, kind):
        n = sum(active(stage, j) for j in range(START, self.i) for _, stage in ORDER[kind])
        return n if self.r is None else self.r * len(ORDER[kind]) + n

    def before(self, kind, use):
        names = [name for name, _ in ORDER[kind]]
        return self.start(kind) + sum(active(stage, self.i) for _, stage in ORDER[kind][:names.index(use)])

    def after(self, kind, use):
        stage = dict(ORDER[kind])[use]
        return self.before(kind, use) + active(stage, self.i)

    def norms(self, slot, later=0):
        for name, at in NORM_SLOT.items():
            if (at + later) % SLOTS == slot:
                stage = dict(ORDER["norm"])[name] if at + later < SLOTS else dict(ORDER["turn"])[name]
                if self.has(stage):
                    yield name

    def times(self, stage, per, k):
        n = per * (self.i - LAG[stage]) + k
        return n if self.r is None else self.r * per + n


def reuse(eng, sem, value):
    if not isinstance(value, int) or value > 0:
        eng.wait_ge(sem, value)


def build(nc, x, wq, bq, wk, bk, wv, bv, w_gate, w_up, w_down, rope, out):
    with ExitStack() as ctx:
        def sb(name, shape, dt=F32):
            return ctx.enter_context(nc.sbuf_tensor(name, shape, dt))

        def bank(name):
            return ctx.enter_context(nc.psum_tensor(name, [P, 512], F32))

        def sem(name):
            return ctx.enter_context(nc.semaphore(name))

        ffn_hi, ffn_lo = sb("ffn_hi", [P, 3, DC * HIDDEN], F32R), sb("ffn_lo", [P, 3, DC * HIDDEN], F32R)
        qkv_hi, qkv_lo = sb("qkv_hi", [P, 3, DC * D], F32R), sb("qkv_lo", [P, 3, DC * D], F32R)
        rope_sb = sb("rope_sb", [P, 2, TOKENS])
        ident = sb("ident", [P, P])
        ones = sb("ones", [P, P])
        ones_r = sb("ones_r", [2, P], F32R)
        qk_bias = sb("qk_bias", [P, 2, DC])
        v_bias = sb("v_bias", [2, D])
        v_bias_lo = sb("v_bias_lo", [1, D], F32R)
        v_bias_parts = sb("v_bias_parts", [2, D], F32R)
        minus_half = sb("minus_half", [P, 2])
        lo_squares = sb("lo_squares", [P, 3])
        lo_total = sb("lo_total", [P, 1])
        wide_flag = sb("wide_flag", [1, 1], I32)
        x_in = sb("x_in", [P, TILES, D])
        x_first = sb("x_first", [P, TILES, D])
        mid = sb("mid", [P, 3, TILES, D])
        x_attend, x_norm3, x_second = (mid[:, n] for n in range(3))
        xn = sb("xn", [P, 2, 2, D])
        bn = sb("bn", [P, 2, 2, 6])
        mean_var = sb("mean_var", [P, 2, 2, 2])
        var_eps, minus_mean = sb("var_eps", [P, 2, 2]), sb("minus_mean", [P, 2, 2])
        minus_twice = sb("minus_twice", [P, 2, 2])
        rstd, shift = sb("rstd", [P, 2, 2]), sb("shift", [P, 2, 2])
        xt_hi = {n: sb(f"xt_hi{n}", [P, DC, TOKENS], F32R) for n in (1, 2, 3)}
        xt_lo = {n: sb(f"xt_lo{n}", [P, DC, TOKENS], F32R) for n in (1, 2, 3)}
        gated = sb("gated", [P, 2, TOKENS])
        hid = sb("hid", [P, 3, TOKENS])
        hid_hi = {f: sb(f"hid_hi_{f}", [P, CHUNKS, TOKENS], F32R) for f in (FIRST, SECOND)}
        hid_lo = {f: sb(f"hid_lo_{f}", [P, CHUNKS, TOKENS], F32R) for f in (FIRST, SECOND)}
        turned_qk = sb("turned_qk", [P, 2, DC, TOKENS])
        cross = sb("cross", [P, DC, TOKENS])
        qk_hi, qk_lo = sb("qk_hi", [P, 2, DC, TOKENS], F32R), sb("qk_lo", [P, 2, DC, TOKENS], F32R)
        v_hi, v_lo = sb("v_hi", [P, TILES, D], F32R), sb("v_lo", [P, TILES, D], F32R)
        minus_max, exp_bias = sb("minus_max", [P, TILES]), sb("exp_bias", [P, TILES])
        prob_sum, prob_inv = sb("prob_sum", [P, TILES]), sb("prob_inv", [P, TILES])
        prob = sb("prob", [P, 2, TOKENS])
        pt_hi, pt_lo = sb("pt_hi", [P, TILES, P], F32R), sb("pt_lo", [P, TILES, P], F32R)

        raw = {
            GATE: mid[:].rearrange("p n t d -> p (n t d)")[:, 0:CHUNKS * D],
            UP: mid[:].rearrange("p n t d -> p (n t d)")[:, CHUNKS * D:2 * CHUNKS * D],
            DOWN: turned_qk[:].rearrange("p n c t -> p (n c t)")[:, 0:DC * HIDDEN],
        }
        raw_qkv = {
            Q: cross[:].rearrange("p c t -> p (c t)")[:, 0:DC * D],
            K: cross[:].rearrange("p c t -> p (c t)")[:, DC * D:2 * DC * D],
            V: turned_qk[:].rearrange("p n c t -> p (n c t)")[:, DC * HIDDEN:DC * HIDDEN + DC * D],
        }

        gate_ps, up_ps = [bank("gate_ps0"), bank("gate_ps1")], [bank("up_ps0"), bank("up_ps1")]
        att_ps = [bank("att_ps0"), bank("att_ps1")]
        turn_ps, out_ps = bank("turn_ps"), bank("out_ps")
        setup_ps = [*gate_ps, *up_ps, *att_ps]

        w_loaded = [sem(f"w_loaded{n}") for n in range(6)]
        const_loaded, made, cast, setup_turned, setup_hi, setup_lo = (
            sem(n) for n in ("const_loaded", "made", "cast", "setup_turned", "setup_hi", "setup_lo"))
        bias_split, bias_placed, squared, total_ready, total_copied, flag_ready = (
            sem(n) for n in ("bias_split", "bias_placed", "squared", "total_ready", "total_copied", "flag_ready"))
        x_loaded, x_first_copied, x_second_copied, stored = (
            sem(n) for n in ("x_loaded", "x_first_copied", "x_second_copied", "stored"))
        bn_done, aggregated, spread_ready, rstd_ready, shift_ready, normed = (
            sem(n) for n in ("bn_done", "aggregated", "spread_ready", "rstd_ready", "shift_ready", "normed"))
        twice_ready = sem("twice_ready")
        turned, turned_hi, turned_lo = sem("turned"), sem("turned_hi"), sem("turned_lo")
        gate_ready, up_ready, tanh_ready, silu_ready, hid_ready, hid_hi_ready, hid_lo_ready = (
            sem(n) for n in ("gate_ready", "up_ready", "tanh_ready", "silu_ready", "hid_ready", "hid_hi_ready", "hid_lo_ready"))
        out_ready, out_taken = sem("out_ready"), sem("out_taken")
        qk_ready, qk_taken, rotated, qk_hi_ready, q_lo_ready, k_lo_ready = (
            sem(n) for n in ("qk_ready", "qk_taken", "rotated", "qk_hi_ready", "q_lo_ready", "k_lo_ready"))
        v_ready, v_hi_ready, v_lo_ready = sem("v_ready"), sem("v_hi_ready"), sem("v_lo_ready")
        score_ready, max_ready, bias_ready, exp_ready, inv_ready = (
            sem(n) for n in ("score_ready", "max_ready", "bias_ready", "exp_ready", "inv_ready"))

        gate_blocks = [raw[GATE].rearrange("p (h d) -> p h d", d=D)[:, h, c * P:(c + 1) * P]
                       for c in range(DC) for h in range(CHUNKS)]
        up_blocks = [raw[UP].rearrange("p (h d) -> p h d", d=D)[:, h, c * P:(c + 1) * P]
                     for c in range(DC) for h in range(CHUNKS)]
        down_blocks = [raw[DOWN].rearrange("p (c q h) -> p c h q", c=DC, h=CHUNKS)[:, c, h, :]
                       for h in range(CHUNKS) for c in range(DC)]
        qkv_blocks = {w: [raw_qkv[w].rearrange("p (c d) -> p c d", c=DC)[:, c, dc * P:(dc + 1) * P]
                          for dc in range(DC) for c in range(DC)] for w in (Q, K, V)}
        groups = []
        for n, blocks in ((GATE, gate_blocks), (UP, up_blocks), (DOWN, down_blocks)):
            for g in range(0, len(blocks), 4):
                groups.append((n, blocks[g:g + 4], ffn_hi[:, n, g * P:(g + 4) * P], ffn_lo[:, n, g * P:(g + 4) * P]))
        for w in (Q, K, V):
            groups.append((3 + w, qkv_blocks[w], qkv_hi[:, w, :], qkv_lo[:, w, :]))
        GROUPS = len(groups)

        norm_source = {"n1": x_in, "n2": x_attend, "n3": x_norm3}
        half = {"a": 0, "b": 1}

        def turned_x(parts, name):
            h = half[name[2]]
            return parts[int(name[1])][:, :, h * 2 * P:(h + 1) * 2 * P]

        def chunk_stage(s):
            return FIRST if s < CHUNKS else SECOND

        def run(eng, iteration, steady_end=STEADY_END):
            for i in range(START, STEADY):
                iteration(Step(i))
            with eng.Fori(0, steady_end - STEADY) as r:
                iteration(Step(STEADY, r))
            for i in range(steady_end, END):
                iteration(Step(i))

        block = ctx.enter_context(nc.Block())

        @block.sync
        def _(sp):
            sp.dma_start(raw[GATE].bitcast(I32), w_gate.rearrange("(p h) d -> p (h d)", h=CHUNKS)).then_inc(w_loaded[GATE], 16)
            sp.dma_start(raw[UP].bitcast(I32), w_up.rearrange("(p h) d -> p (h d)", h=CHUNKS)).then_inc(w_loaded[UP], 16)
            sp.dma_start(x_in[:], x[0].rearrange("(p t) d -> p t d", t=TILES)).then_inc(x_loaded, 16)
            sp.dma_start(raw[DOWN].bitcast(I32).rearrange("p (c n) -> p c n", c=DC),
                         w_down.rearrange("(c p) n -> p c n", p=P)).then_inc(w_loaded[DOWN], 16)
            sp.wait_ge(bias_split, 2)
            sp.dma_start(v_bias_parts[1:2, :].bitcast(F32), v_bias_lo[0:1, :].bitcast(F32)).then_inc(bias_placed, 16)

            def batch(s, stage, later=0):
                n = s.i - LAG[stage] + later
                return n if s.r is None else sp.snap(s.r + n)

            def iteration(s):
                if s.has(SECOND_DOWN):
                    finished = out[batch(s, SECOND_DOWN)].rearrange("(p t) d -> p t d", t=TILES)
                    sp.wait_ge(out_taken, s.after("out", "second3"))
                    sp.dma_start(finished, x_second).then_inc(stored, 16)
                if s.has(SECOND):
                    if s.has(SECOND_DOWN):
                        sp.wait_ge(stored, s.times(SECOND_DOWN, 16, 16))
                    else:
                        sp.wait_ge(normed, s.after("norm", "n3b"))
                    sp.dma_start(x_second, x_norm3).then_inc(x_second_copied, 16)
                if s.has(AHEAD):
                    if s.has(FIRST):
                        sp.wait_ge(out_taken, s.after("out", "first3"))
                    else:
                        sp.wait_ge(normed, s.after("norm", "n1b"))
                    sp.dma_start(x_first[:], x_in[:]).then_inc(x_first_copied, 16)
                if active(AHEAD, s.i + 1):
                    coming = x[batch(s, AHEAD, 1)].rearrange("(p t) d -> p t d", t=TILES)
                    sp.wait_ge(x_first_copied, s.times(AHEAD, 16, 16))
                    sp.dma_start(x_in[:], coming).then_inc(x_loaded, 16)

            run(sp, iteration, STEADY_END - 1)
            sp.wait_ge(stored, 16 * BATCHES)

        @block.gpsimd
        def _(pool):
            pool.memset(ident[:], 0.0).then_inc(made, 1)
            pool.memset(ones[:], 1.0).then_inc(made, 1)
            pool.memset(minus_half[:], -0.5).then_inc(made, 1)
            pool.wait_ge(made, 1)
            pool.affine_select(out=ident[:], in_=ident[:], compare_op=ALU.not_equal, fill=1.0,
                               base=0, pattern=[[-1, P]], channel_multiplier=1).then_inc(made, 1)

            def inverse_std(s, name):
                h = half[name[2]]
                n = s.before("norm", name)
                pool.wait_ge(spread_ready, (n + 1) * 2)
                nc.gpsimd.tensor_tensor(rstd[:, h], var_eps[:, h], minus_half[:], ALU.pow).then_inc(rstd_ready, 1)
                pool.wait_ge(rstd_ready, n + 1)
                nc.gpsimd.tensor_tensor(shift[:, h], minus_mean[:, h], rstd[:, h], ALU.mult).then_inc(shift_ready, 1)

            def hidden_lo(s, slot):
                n = s.before("chunk", slot)
                f = chunk_stage(slot)
                pool.wait_ge(hid_hi_ready, n + 1)
                nc.gpsimd.tensor_tensor(hid_lo[f][:, slot % CHUNKS], hid[:, slot % 3],
                                        hid_hi[f][:, slot % CHUNKS].bitcast(F32), ALU.subtract).then_inc(hid_lo_ready, 1)

            def rotate(s, w):
                pool.wait_ge(qk_taken, s.times(ATTEND, 2, w + 1))
                nc.gpsimd.tensor_tensor(turned_qk[:, w, 0], turned_qk[:, w, 0], cross[:, 0], ALU.subtract)
                nc.gpsimd.tensor_tensor(turned_qk[:, w, 1], turned_qk[:, w, 1], cross[:, 1], ALU.add).then_inc(rotated, 1)

            def query_lo(s):
                pool.wait_ge(qk_hi_ready, s.times(ATTEND, 2, 1))
                nc.gpsimd.tensor_tensor(qk_lo[:, Q], turned_qk[:, Q], qk_hi[:, Q].bitcast(F32),
                                        ALU.subtract).then_inc(q_lo_ready, 1)

            def iteration(s):
                for slot in range(SLOTS):
                    if s.has(chunk_stage(slot)):
                        hidden_lo(s, slot)
                    for name in s.norms(slot):
                        inverse_std(s, name)
                    if slot == 1 and s.has(ATTEND):
                        rotate(s, Q)
                    if slot == 2 and s.has(ATTEND):
                        rotate(s, K)
                    if slot == 3 and s.has(ATTEND):
                        query_lo(s)

            run(pool, iteration)

        @block.scalar
        def _(act):
            for w, weight in ((Q, wq), (K, wk)):
                act.dma_start(raw_qkv[w], weight.rearrange("(p c) d -> p (c d)", c=DC)).then_inc(w_loaded[3 + w], 16)
            act.dma_start(raw_qkv[V].rearrange("p (c d) -> p c d", c=DC),
                          wv.rearrange("(c p) d -> p c d", p=P)).then_inc(w_loaded[3 + V], 16)
            act.dma_start(rope_sb[:], rope.rearrange("n p t -> p n t")).then_inc(const_loaded, 16)
            for w, bias in ((Q, bq), (K, bk)):
                act.dma_start(qk_bias[:, w], bias.rearrange("(p c) -> p c", c=DC)).then_inc(const_loaded, 16)
            for row in range(2):
                act.dma_start(v_bias[row:row + 1, :], bv.rearrange("(a d) -> a d", a=1)).then_inc(const_loaded, 16)

            for g, (_, _, hi, _) in enumerate(groups):
                act.wait_ge(setup_turned, g + 1)
                nc.scalar.activation(hi, setup_ps[g % len(setup_ps)][:], ACT.Copy).then_inc(setup_hi, 1)
            act.wait_ge(setup_lo, GROUPS)
            for n, scratch in ((GATE, raw[GATE]), (UP, raw[UP]), (DOWN, raw[DOWN])):
                nc.scalar.activation(scratch, ffn_lo[:, n].bitcast(F32), ACT.Square,
                                     accum_out=lo_squares[:, n:n + 1]).then_inc(squared, 1)

            def normalise(s, name):
                n = s.before("norm", name)
                h = half[name[2]]
                act.wait_ge(shift_ready, n + 1)
                before = {"n3a": s.start("turn"), "n3b": s.after("turn", "n2b"), "n1a": s.after("turn", "n3a"),
                          "n1b": s.after("turn", "n3b"), "n2a": s.after("turn", "n1a"), "n2b": s.after("turn", "n1b")}[name]
                reuse(act, turned, before)
                for u in range(2):
                    last = nc.scalar.activation(xn[:, h, u], norm_source[name[:2]][:, 2 * h + u], ACT.Identity,
                                                bias=shift[:, h, u:u + 1], scale=rstd[:, h, u:u + 1])
                last.then_inc(normed, 1)

            def norm_hi(s, name):
                act.wait_ge(turned, s.before("turn", name) + 1)
                if name[:2] == "n1":
                    reuse(act, up_ready, s.after("chunk", CHUNKS - 1))
                elif name == "n2a":
                    reuse(act, v_ready, s.times(FIRST, 2, 0))
                elif name == "n3a":
                    reuse(act, up_ready, s.start("chunk"))
                nc.scalar.activation(turned_x(xt_hi, name), turn_ps[:].rearrange("p (c t) -> p c t", c=DC),
                                     ACT.Copy).then_inc(turned_hi, 1)

            def tanh(s, slot):
                act.wait_ge(gate_ready, s.before("chunk", slot) + 1)
                nc.scalar.activation(gated[:, slot % 2], gate_ps[slot % 2][:], ACT.Tanh,
                                     scale=0.5 * WEIGHT_SCALE).then_inc(tanh_ready, 1)

            def hidden_hi(s, slot):
                f = chunk_stage(slot)
                act.wait_ge(hid_ready, s.before("chunk", slot) + 1)
                if slot == 0:
                    reuse(act, out_ready, s.start("out"))
                if slot == CHUNKS:
                    reuse(act, out_ready, s.after("out", "second3"))
                nc.scalar.activation(hid_hi[f][:, slot % CHUNKS], hid[:, slot % 3], ACT.Copy).then_inc(hid_hi_ready, 1)

            def rotated_hi(s, w):
                act.wait_ge(rotated, s.times(ATTEND, 2, w + 1))
                nc.scalar.activation(qk_hi[:, w], turned_qk[:, w], ACT.Copy).then_inc(qk_hi_ready, 1)

            def values_hi(s, pair):
                if pair == 0:
                    reuse(act, out_ready, s.start("out"))
                act.wait_ge(v_ready, s.times(ATTEND, 2, pair + 1))
                nc.scalar.activation(v_hi[:, 2 * pair:2 * pair + 2], att_ps[pair][:].rearrange("p (u d) -> p u d", u=2),
                                     ACT.Copy).then_inc(v_hi_ready, 1)

            def exponent(s, t):
                reuse(act, turned, s.start("turn") if t < 2 else s.after("turn", f"p{t - 2}"))
                act.wait_ge(bias_ready, s.times(ATTEND, TILES, t + 1))
                nc.scalar.activation(prob[:, t % 2], att_ps[t % 2][:], ACT.Exp, bias=exp_bias[:, t:t + 1],
                                     scale=D ** -0.5, accum_out=prob_sum[:, t:t + 1]).then_inc(exp_ready, 1)

            def prob_hi(s, t):
                act.wait_ge(turned, s.before("turn", f"p{t}") + 1)
                reuse(act, out_ready, s.start("out") if t == 0 else s.after("out", f"attend{t - 1}"))
                nc.scalar.activation(pt_hi[:], turn_ps[:].rearrange("p (k q) -> p k q", k=TILES),
                                     ACT.Copy).then_inc(turned_hi, 1)

            def iteration(s):
                attend = s.has(ATTEND)
                for slot in range(SLOTS):
                    if s.has(chunk_stage(slot)):
                        tanh(s, slot)
                    for name in s.norms(slot, 1):
                        normalise(s, name)
                    for name in s.norms(slot, 2):
                        norm_hi(s, name)
                    if s.has(chunk_stage(slot)):
                        hidden_hi(s, slot)
                    if attend and slot == 2:
                        rotated_hi(s, Q)
                    if attend and slot == 3:
                        values_hi(s, 0)
                        values_hi(s, 1)
                    if attend and slot == 4:
                        rotated_hi(s, K)
                    if attend and 6 <= slot < 6 + TILES:
                        prob_hi(s, slot - 6)
                    if attend and 5 <= slot < 5 + TILES:
                        exponent(s, slot - 5)

            run(act, iteration)

        @block.vector
        def _(dve):
            for n in (GATE, UP, DOWN):
                dve.wait_ge(w_loaded[n], 16)
                nc.vector.tensor_copy(raw[n], raw[n].bitcast(I32)).then_inc(cast, 1)
            dve.wait_ge(made, 4)
            nc.vector.tensor_copy(ones_r[:], ones[0:2, :]).then_inc(bias_split, 1)
            dve.wait_ge(const_loaded, 16 * 5)
            nc.vector.tensor_copy(v_bias_parts[0:1, :], v_bias[0:1, :]).then_inc(cast, 1)
            dve.wait_ge(cast, 4)
            nc.vector.tensor_tensor(v_bias_lo[0:1, :], v_bias[0:1, :], v_bias_parts[0:1, :].bitcast(F32),
                                    ALU.subtract).then_inc(bias_split, 1)
            for g, (_, _, hi, lo) in enumerate(groups):
                dve.wait_ge(setup_hi, g + 1)
                nc.vector.tensor_tensor(lo, setup_ps[g % len(setup_ps)][:], hi.bitcast(F32), ALU.subtract).then_inc(setup_lo, 1)
            dve.wait_ge(squared, 3)
            nc.vector.tensor_reduce(lo_total[:], lo_squares[:], AX_X, ALU.add).then_inc(total_ready, 1)
            dve.wait_ge(total_copied, 1)
            nc.vector.tensor_scalar(wide_flag[:], out_ps[0:1, 0:1], 1.0, None, ALU.min).then_inc(flag_ready, 1)

            def statistics(s, name):
                n = s.before("norm", name)
                h = half[name[2]]
                if name == "n1a":
                    dve.wait_ge(x_loaded, s.times(AHEAD, 16, 16))
                elif name == "n3a":
                    dve.wait_ge(out_taken, s.start("out"))
                elif name in ("n2a", "n2b"):
                    dve.wait_ge(out_taken, s.after("out", "first1" if name == "n2a" else "first3"))
                reuse(dve, normed, n - 1)
                for u in range(2):
                    last = nc.vector.bn_stats(bn[:, h, u], norm_source[name[:2]][:, 2 * h + u])
                last.then_inc(bn_done, 1)
                dve.wait_ge(bn_done, n + 1)
                nc.vector.scalar_tensor_tensor(minus_twice[:, h], bn[:, h, :, 1], -1.0, bn[:, h, :, 4],
                                               ALU.mult, ALU.subtract).then_inc(twice_ready, 1)
                for u in range(2):
                    last = nc.vector.bn_aggr(mean_var[:, h, u], bn[:, h, u])
                last.then_inc(aggregated, 1)
                dve.wait_ge(aggregated, n + 1)
                nc.vector.tensor_scalar(var_eps[:, h], mean_var[:, h, :, 1], EPS, None, ALU.add).then_inc(spread_ready, 1)
                dve.wait_ge(twice_ready, n + 1)
                nc.vector.tensor_scalar(minus_mean[:, h], minus_twice[:, h], 0.5, None, ALU.mult).then_inc(spread_ready, 1)

            def norm_lo(s, name):
                dve.wait_ge(turned_hi, s.before("turn", name) + 1)
                nc.vector.tensor_tensor(turned_x(xt_lo, name), turn_ps[:].rearrange("p (c t) -> p c t", c=DC),
                                        turned_x(xt_hi, name).bitcast(F32), ALU.subtract).then_inc(turned_lo, 1)

            def silu(s, slot):
                n = s.before("chunk", slot)
                dve.wait_ge(tanh_ready, n + 1)
                nc.vector.scalar_tensor_tensor(gated[:, slot % 2], gated[:, slot % 2], 1.0, gate_ps[slot % 2][:],
                                               ALU.add, ALU.mult).then_inc(silu_ready, 1)

            def hidden(s, slot):
                n = s.before("chunk", slot)
                dve.wait_ge(silu_ready, n + 1)
                dve.wait_ge(up_ready, n + 1)
                reuse(dve, hid_lo_ready, n - 2)
                nc.vector.tensor_tensor(hid[:, slot % 3], gated[:, slot % 2], up_ps[slot % 2][:],
                                        ALU.mult).then_inc(hid_ready, 1)

            def rope_products(s, w):
                dve.wait_ge(qk_ready, s.times(ATTEND, 2, w + 1))
                if w == K:
                    dve.wait_ge(rotated, s.times(ATTEND, 2, 1))
                cos, sin = rope_sb[:, 0], rope_sb[:, 1]
                for ps, c, table, product in ((att_ps[0], 0, cos, turned_qk[:, w, 0]), (att_ps[0], 0, sin, turned_qk[:, w, 1]),
                                              (att_ps[1], 1, sin, cross[:, 0]), (att_ps[1], 1, cos, cross[:, 1])):
                    last = nc.vector.scalar_tensor_tensor(product, ps[:], qk_bias[:, w, c:c + 1], table, ALU.add, ALU.mult)
                last.then_inc(qk_taken, 1)

            def key_lo(s):
                dve.wait_ge(qk_hi_ready, s.times(ATTEND, 2, 2))
                nc.vector.tensor_tensor(qk_lo[:, K], turned_qk[:, K], qk_hi[:, K].bitcast(F32),
                                        ALU.subtract).then_inc(k_lo_ready, 1)

            def values_lo(s, pair):
                dve.wait_ge(v_hi_ready, s.times(ATTEND, 2, pair + 1))
                nc.vector.tensor_tensor(v_lo[:, 2 * pair:2 * pair + 2], att_ps[pair][:].rearrange("p (u d) -> p u d", u=2),
                                        v_hi[:, 2 * pair:2 * pair + 2].bitcast(F32), ALU.subtract).then_inc(v_lo_ready, 1)

            def row_max(s, t):
                dve.wait_ge(score_ready, s.times(ATTEND, TILES, t + 1))
                nc.vector.tensor_reduce(minus_max[:, t:t + 1], att_ps[t % 2][:], AX_X, ALU.max,
                                        negate=True).then_inc(max_ready, 1)
                dve.wait_ge(max_ready, s.times(ATTEND, TILES, t + 1))
                nc.vector.tensor_scalar(exp_bias[:, t:t + 1], minus_max[:, t:t + 1], D ** -0.5, None,
                                        ALU.mult).then_inc(bias_ready, 1)

            def prob_lo(s, t):
                dve.wait_ge(turned_hi, s.before("turn", f"p{t}") + 1)
                nc.vector.tensor_tensor(pt_lo[:], turn_ps[:].rearrange("p (k q) -> p k q", k=TILES),
                                        pt_hi[:].bitcast(F32), ALU.subtract).then_inc(turned_lo, 1)
                nc.vector.reciprocal(prob_inv[:, t:t + 1], prob_sum[:, t:t + 1]).then_inc(inv_ready, 1)

            def attended(s, t):
                dve.wait_ge(out_ready, s.before("out", f"attend{t}") + 1)
                dve.wait_ge(inv_ready, s.times(ATTEND, TILES, t + 1))
                if t == 0:
                    reuse(dve, x_second_copied, s.times(ATTEND, 16, 0))
                nc.vector.scalar_tensor_tensor(x_norm3[:, t], out_ps[:, 0:D], prob_inv[:, t:t + 1], x_attend[:, t],
                                               ALU.mult, ALU.add).then_inc(out_taken, 1)

            def fed(s, stage, t, name, source, target):
                dve.wait_ge(out_ready, s.before("out", f"{name}{t}") + 1)
                if t == 0 and stage == FIRST:
                    dve.wait_ge(x_first_copied, s.times(FIRST, 16, 16))
                if t == 0 and stage == SECOND_DOWN:
                    dve.wait_ge(x_second_copied, s.times(SECOND_DOWN, 16, 16))
                nc.vector.scalar_tensor_tensor(target[:, t], out_ps[:, 0:D], 0.25 * WEIGHT_SCALE ** 3, source[:, t],
                                               ALU.mult, ALU.add).then_inc(out_taken, 1)

            def iteration(s):
                attend = s.has(ATTEND)
                for slot in range(SLOTS):
                    if s.has(chunk_stage(slot)):
                        silu(s, slot)
                    if attend and 7 <= slot < 7 + TILES:
                        attended(s, slot - 7)
                    if s.has(chunk_stage(slot)):
                        hidden(s, slot)
                    for name in s.norms(slot, 2):
                        norm_lo(s, name)
                    if s.has(SECOND_DOWN) and 1 <= slot < 1 + TILES:
                        fed(s, SECOND_DOWN, slot - 1, "second", x_second, x_second)
                    if s.has(FIRST) and 7 <= slot < 7 + TILES:
                        fed(s, FIRST, slot - 7, "first", x_first, x_attend)
                    if attend and 6 <= slot < 6 + TILES:
                        prob_lo(s, slot - 6)
                    if attend and slot == 1:
                        rope_products(s, Q)
                    if attend and slot == 2:
                        rope_products(s, K)
                    if attend and slot == 3:
                        values_lo(s, 0)
                        values_lo(s, 1)
                    if attend and slot == 4:
                        key_lo(s)
                    if attend and 5 <= slot < 5 + TILES:
                        row_max(s, slot - 5)
                    for name in s.norms(slot):
                        statistics(s, name)

            run(dve, iteration)

        @block.tensor
        def _(pe):
            pe.wait_ge(made, 4)
            for g, (weight, blocks, _, _) in enumerate(groups):
                if weight < 3:
                    pe.wait_ge(cast, weight + 1)
                else:
                    pe.wait_ge(w_loaded[weight], 16)
                reuse(pe, setup_lo, g - len(setup_ps) + 1)
                for n, b in enumerate(blocks):
                    last = nc.tensor.transpose(setup_ps[g % len(setup_ps)][:, n * P:(n + 1) * P], b, ident[:])
                last.then_inc(setup_turned, 1)
            pe.wait_ge(total_ready, 1)
            nc.tensor.matmul(out_ps[0:1, 0:1], lo_total[:], ones[:, 0:1], start=True, stop=True).then_inc(total_copied, 1)
            pe.wait_ge(bias_split, 2)
            pe.wait_ge(bias_placed, 16)
            pe.wait_ge(const_loaded, 16 * 5)
            pe.wait_ge(flag_ready, 1)
            wide = pe.value_load(wide_flag[0:1, 0:1], min_val=0, max_val=1)

            def products(out, terms):
                for n, (lhs_t, rhs) in enumerate(terms):
                    last = nc.tensor.matmul(out, lhs_t, rhs, start=(n == 0), stop=(n == len(terms) - 1))
                return last

            def program(ffn_passes):
                def norm_turn(s, name):
                    h = half[name[2]]
                    pe.wait_ge(normed, s.start("norm") if name == "n2b" else s.after("norm", name))
                    reuse(pe, turned_lo, s.before("turn", name))
                    for u in range(2):
                        for c in range(DC):
                            last = nc.tensor.transpose(turn_ps[:, c * 2 * P + u * P:c * 2 * P + (u + 1) * P],
                                                       xn[:, h, u, c * P:(c + 1) * P], ident[:])
                    last.then_inc(turned, 1)

                def chunk(s, slot, w, ps, ready):
                    n = s.before("chunk", slot)
                    h = slot % CHUNKS
                    norm = 1 if slot < CHUNKS else 3
                    if w == GATE and h == 0:
                        pe.wait_ge(turned_lo, s.start("turn") if norm == 1 else s.after("turn", "n3b"))
                    if w == GATE:
                        reuse(pe, hid_ready, n - 1)
                    terms = []
                    for c in range(DC):
                        hi, lo = (part[:, w, c * HIDDEN + h * P:c * HIDDEN + (h + 1) * P] for part in (ffn_hi, ffn_lo))
                        terms += [(hi, xt_hi[norm][:, c]), (hi, xt_lo[norm][:, c]), (lo, xt_hi[norm][:, c])][:ffn_passes]
                    products(ps[slot % 2][:], terms).then_inc(ready, 1)

                def down(s, f, name, t, chunks_done):
                    if t == 0:
                        pe.wait_ge(hid_lo_ready, chunks_done)
                    reuse(pe, out_taken, s.before("out", f"{name}{t}"))
                    terms = []
                    for h in range(CHUNKS):
                        hi, lo = (part[f][:, h, t * P:(t + 1) * P] for part in (hid_hi, hid_lo))
                        w_hi, w_lo = (part[:, DOWN, h * D:(h + 1) * D] for part in (ffn_hi, ffn_lo))
                        terms += [(hi, w_hi), (lo, w_hi), (hi, w_lo)][:ffn_passes]
                    products(out_ps[:, 0:D], terms).then_inc(out_ready, 1)

                def project(s, w):
                    if w == Q:
                        pe.wait_ge(turned_lo, s.after("turn", "n2b"))
                        reuse(pe, exp_ready, s.times(ATTEND, TILES, 0))
                    else:
                        pe.wait_ge(qk_taken, s.times(ATTEND, 2, 1))
                    for c in range(DC):
                        terms = []
                        for dc in range(DC):
                            hi, lo = (part[:, w, (dc * DC + c) * P:(dc * DC + c + 1) * P] for part in (qkv_hi, qkv_lo))
                            terms += [(hi, xt_hi[2][:, dc]), (hi, xt_lo[2][:, dc]), (lo, xt_hi[2][:, dc])]
                        last = products(att_ps[c][:], terms)
                    last.then_inc(qk_ready, 1)

                def values(s, pair):
                    pe.wait_ge(qk_taken, s.times(ATTEND, 2, 2))
                    for u in range(2):
                        at = (2 * pair + u) * P
                        terms = [(ones_r[:], v_bias_parts[:])]
                        for dc in range(DC):
                            hi, lo = (part[:, V, dc * D:(dc + 1) * D] for part in (qkv_hi, qkv_lo))
                            x_hi, x_lo = xt_hi[2][:, dc, at:at + P], xt_lo[2][:, dc, at:at + P]
                            terms += [(x_hi, hi), (x_hi, lo), (x_lo, hi)]
                        last = products(att_ps[pair][:, u * D:(u + 1) * D], terms)
                    last.then_inc(v_ready, 1)

                def scores(s, t):
                    if t == 0:
                        pe.wait_ge(q_lo_ready, s.times(ATTEND, 1, 1))
                        pe.wait_ge(k_lo_ready, s.times(ATTEND, 1, 1))
                    if t < 2:
                        pe.wait_ge(v_lo_ready, s.times(ATTEND, 2, t + 1))
                    else:
                        pe.wait_ge(exp_ready, s.times(ATTEND, TILES, t - 1))
                    terms = []
                    for c in range(DC):
                        q_hi, q_lo = (part[:, Q, c, t * P:(t + 1) * P] for part in (qk_hi, qk_lo))
                        terms += [(q_hi, qk_hi[:, K, c]), (q_hi, qk_lo[:, K, c]), (q_lo, qk_hi[:, K, c])]
                    products(att_ps[t % 2][:], terms).then_inc(score_ready, 1)

                def prob_turn(s, t):
                    pe.wait_ge(exp_ready, s.times(ATTEND, TILES, t + 1))
                    reuse(pe, turned_lo, s.before("turn", f"p{t}"))
                    for k in range(TILES):
                        last = nc.tensor.transpose(turn_ps[:, k * P:(k + 1) * P], prob[:, t % 2, k * P:(k + 1) * P], ident[:])
                    last.then_inc(turned, 1)

                def weigh(s, t):
                    pe.wait_ge(turned_lo, s.after("turn", f"p{t}"))
                    reuse(pe, out_taken, s.before("out", f"attend{t}"))
                    terms = []
                    for k in range(TILES):
                        terms += [(pt_hi[:, k], v_hi[:, k]), (pt_hi[:, k], v_lo[:, k]), (pt_lo[:, k], v_hi[:, k])]
                    products(out_ps[:, 0:D], terms).then_inc(out_ready, 1)

                def iteration(s):
                    attend = s.has(ATTEND)
                    for slot in range(SLOTS):
                        if s.has(chunk_stage(slot)):
                            chunk(s, slot, GATE, gate_ps, gate_ready)
                        if attend and 7 <= slot < 7 + TILES:
                            weigh(s, slot - 7)
                        if s.has(chunk_stage(slot)):
                            chunk(s, slot, UP, up_ps, up_ready)
                        for name in s.norms(slot, 2):
                            norm_turn(s, name)
                        if s.has(SECOND_DOWN) and 1 <= slot < 1 + TILES:
                            down(s, SECOND, "second", slot - 1, s.start("chunk"))
                        if s.has(FIRST) and 7 <= slot < 7 + TILES:
                            down(s, FIRST, "first", slot - 7, s.after("chunk", CHUNKS - 1))
                        if attend and 6 <= slot < 6 + TILES:
                            prob_turn(s, slot - 6)
                        if attend and slot == 1:
                            project(s, Q)
                        if attend and slot == 2:
                            project(s, K)
                        if attend and slot == 3:
                            values(s, 0)
                            values(s, 1)
                        if attend and 5 <= slot < 5 + TILES:
                            scores(s, slot - 5)

                run(pe, iteration)

            with pe.If(wide > 0):
                program(3)
            with pe.Else():
                program(2)


def rope_tables():
    inv_freq = (1.0 / np.float32(THETA) ** (np.arange(0, D, 2, dtype=np.float32) / np.float32(D))).astype(np.float32)
    token = np.arange(TOKENS).reshape(P, TILES).T.reshape(-1).astype(np.float32)
    angle = inv_freq[:, None] * token[None, :]
    return np.stack([np.cos(angle), np.sin(angle)]).astype(np.float32)


INPUTS = ["L0_attn_x", "L0_attn_wq_w", "L0_attn_wq_b", "L0_attn_wk_w", "L0_attn_wk_b", "L0_attn_wv_w",
          "L0_attn_wv_b", "L0_ffn_w_gate", "L0_ffn_w_up", "L0_ffn_w_down"]


def kernel(**inputs):
    import concourse.bacc as bacc
    from concourse.bass_utils import run_bass_kernel_spmd

    nc = bacc.Bacc("TRN2", target_bir_lowering=False, num_devices=1)
    arrays = {name: np.ascontiguousarray(inputs[name]) for name in INPUTS}
    arrays["rope"] = rope_tables()
    args = [nc.dram_tensor(f"in_{name}", a.shape, mybir.dt.from_np(a.dtype), kind="ExternalInput").ap()
            for name, a in arrays.items()]
    out = nc.dram_tensor("out", (BATCHES, TOKENS, D), F32, kind="ExternalOutput").ap()
    build(nc, *args, out)
    result = run_bass_kernel_spmd(nc, [{f"in_{name}": a for name, a in arrays.items()}], core_ids=[0])
    return result.results[0]["out"]
```

```python
from contextlib import ExitStack

import numpy as np

import concourse.bass as bass
from concourse import mybir

F32 = mybir.dt.float32
F32R = mybir.dt.float32r
I32 = mybir.dt.int32
ALU = mybir.AluOpType
ACT = mybir.ActivationFunctionType
AX_X = mybir.AxisListType.X

P = 128
BATCHES, TOKENS, D = 16, 512, 256
HIDDEN = 768
TILES = TOKENS // P
DC = D // P
CHUNKS = HIDDEN // P
SLOTS = 2 * CHUNKS
EPS = 1e-5
THETA = 10000.0
WEIGHT_SCALE = 1.0 / 127.0
GATE, UP, DOWN = range(3)
Q, K, V = range(3)

FIRST, ATTEND, SECOND, SECOND_DOWN, AHEAD = "first", "attend", "second", "second_down", "ahead"
LAG = {AHEAD: -1, FIRST: 0, ATTEND: 1, SECOND: 2, SECOND_DOWN: 3}
START, STEADY, STEADY_END, END = -1, 4, 15, BATCHES + 3

ORDER = {
    "chunk": [(s, FIRST if s < CHUNKS else SECOND) for s in range(SLOTS)],
    "norm": [("n3a", SECOND), ("n3b", SECOND), ("n1a", AHEAD), ("n1b", AHEAD), ("n2a", FIRST), ("n2b", FIRST)],
    "turn": [("n2b", ATTEND), ("n3a", SECOND), ("n3b", SECOND), ("n1a", AHEAD),
             ("p0", ATTEND), ("n1b", AHEAD), ("p1", ATTEND),
             ("p2", ATTEND), ("n2a", FIRST), ("p3", ATTEND)],
    "out": [("second0", SECOND_DOWN), ("second1", SECOND_DOWN), ("second2", SECOND_DOWN), ("second3", SECOND_DOWN),
            ("first0", FIRST), ("attend0", ATTEND), ("first1", FIRST), ("attend1", ATTEND),
            ("first2", FIRST), ("attend2", ATTEND), ("first3", FIRST), ("attend3", ATTEND)],
}


STATISTICS, APPLY, TURN = range(3)
NORM_SLOTS = {"n3a": (0, 1, 3), "n3b": (2, 3, 4), "n1a": (3, 5, 6), "n1b": (5, 7, 8),
              "n2a": (8, 9, 10), "n2b": (10, 11, 12)}
EARLY = ('n3b',)


def active(stage, i):
    return 0 <= i - LAG[stage] < BATCHES


class Step:

    def __init__(self, i, r=None):
        self.i, self.r = i, r

    def has(self, stage):
        return active(stage, self.i)

    def start(self, kind):
        n = sum(active(stage, j) for j in range(START, self.i) for _, stage in ORDER[kind])
        return n if self.r is None else self.r * len(ORDER[kind]) + n

    def before(self, kind, use):
        names = [name for name, _ in ORDER[kind]]
        return self.start(kind) + sum(active(stage, self.i) for _, stage in ORDER[kind][:names.index(use)])

    def after(self, kind, use):
        stage = dict(ORDER[kind])[use]
        return self.before(kind, use) + active(stage, self.i)

    def norms(self, slot, step):
        for name, slots in NORM_SLOTS.items():
            if slots[step] % SLOTS == slot:
                stage = dict(ORDER["norm"])[name] if slots[step] < SLOTS else dict(ORDER["turn"])[name]
                if self.has(stage):
                    yield name

    def times(self, stage, per, k):
        n = per * (self.i - LAG[stage]) + k
        return n if self.r is None else self.r * per + n


def reuse(eng, sem, value):
    if not isinstance(value, int) or value > 0:
        eng.wait_ge(sem, value)


def build(nc, x, wq, bq, wk, bk, wv, bv, w_gate, w_up, w_down, rope, out):
    with ExitStack() as ctx:
        def sb(name, shape, dt=F32):
            return ctx.enter_context(nc.sbuf_tensor(name, shape, dt))

        def bank(name):
            return ctx.enter_context(nc.psum_tensor(name, [P, 512], F32))

        def sem(name):
            return ctx.enter_context(nc.semaphore(name))

        ffn_hi, ffn_lo = sb("ffn_hi", [P, 3, DC * HIDDEN], F32R), sb("ffn_lo", [P, 3, DC * HIDDEN], F32R)
        qkv_hi, qkv_lo = sb("qkv_hi", [P, 3, DC * D], F32R), sb("qkv_lo", [P, 3, DC * D], F32R)
        rope_sb = sb("rope_sb", [P, 2, TOKENS])
        ident = sb("ident", [P, P])
        ones = sb("ones", [P, P])
        ones_r = sb("ones_r", [2, P], F32R)
        qk_bias = sb("qk_bias", [P, 2, DC])
        v_bias = sb("v_bias", [2, D])
        v_bias_lo = sb("v_bias_lo", [1, D], F32R)
        v_bias_parts = sb("v_bias_parts", [2, D], F32R)
        minus_half = sb("minus_half", [P, 2])
        lo_squares = sb("lo_squares", [P, 3])
        lo_total = sb("lo_total", [P, 1])
        wide_flag = sb("wide_flag", [1, 1], I32)
        x_in = sb("x_in", [P, TILES, D])
        x_first = sb("x_first", [P, TILES, D])
        mid = sb("mid", [P, 3, TILES, D])
        x_attend, x_norm3, x_second = (mid[:, n] for n in range(3))
        xn = sb("xn", [P, 2, 2, D])
        bn = sb("bn", [P, 2, 2, 6])
        mean_var = sb("mean_var", [P, 2, 2, 2])
        var_eps, minus_mean = sb("var_eps", [P, 2, 2]), sb("minus_mean", [P, 2, 2])
        minus_twice = sb("minus_twice", [P, 2, 2])
        rstd, shift = sb("rstd", [P, 2, 2]), sb("shift", [P, 2, 2])
        xt_hi = {n: sb(f"xt_hi{n}", [P, DC, TOKENS], F32R) for n in (1, 2, 3)}
        xt_lo = {n: sb(f"xt_lo{n}", [P, DC, TOKENS], F32R) for n in (1, 2, 3)}
        gated = sb("gated", [P, 2, TOKENS])
        hid = sb("hid", [P, 3, TOKENS])
        hid_hi = {f: sb(f"hid_hi_{f}", [P, CHUNKS, TOKENS], F32R) for f in (FIRST, SECOND)}
        hid_lo = {f: sb(f"hid_lo_{f}", [P, CHUNKS, TOKENS], F32R) for f in (FIRST, SECOND)}
        turned_qk = sb("turned_qk", [P, 2, DC, TOKENS])
        cross = sb("cross", [P, DC, TOKENS])
        qk_hi, qk_lo = sb("qk_hi", [P, 2, DC, TOKENS], F32R), sb("qk_lo", [P, 2, DC, TOKENS], F32R)
        v_hi, v_lo = sb("v_hi", [P, TILES, D], F32R), sb("v_lo", [P, TILES, D], F32R)
        minus_max, exp_bias = sb("minus_max", [P, TILES]), sb("exp_bias", [P, TILES])
        prob_sum, prob_inv = sb("prob_sum", [P, TILES]), sb("prob_inv", [P, TILES])
        prob = sb("prob", [P, 2, TOKENS])
        pt_hi, pt_lo = sb("pt_hi", [P, TILES, P], F32R), sb("pt_lo", [P, TILES, P], F32R)

        raw = {
            GATE: mid[:].rearrange("p n t d -> p (n t d)")[:, 0:CHUNKS * D],
            UP: mid[:].rearrange("p n t d -> p (n t d)")[:, CHUNKS * D:2 * CHUNKS * D],
            DOWN: turned_qk[:].rearrange("p n c t -> p (n c t)")[:, 0:DC * HIDDEN],
        }
        raw_qkv = {
            Q: cross[:].rearrange("p c t -> p (c t)")[:, 0:DC * D],
            K: cross[:].rearrange("p c t -> p (c t)")[:, DC * D:2 * DC * D],
            V: turned_qk[:].rearrange("p n c t -> p (n c t)")[:, DC * HIDDEN:DC * HIDDEN + DC * D],
        }

        gate_ps, up_ps = [bank("gate_ps0"), bank("gate_ps1")], [bank("up_ps0"), bank("up_ps1")]
        att_ps = [bank("att_ps0"), bank("att_ps1")]
        turn_ps, out_ps = bank("turn_ps"), bank("out_ps")
        setup_ps = [*gate_ps, out_ps, *att_ps, *up_ps]

        w_loaded = [sem(f"w_loaded{n}") for n in range(6)]
        const_loaded, made, cast, setup_turned, setup_hi, setup_lo = (
            sem(n) for n in ("const_loaded", "made", "cast", "setup_turned", "setup_hi", "setup_lo"))
        bias_split, bias_placed, squared, total_ready, total_copied, flag_ready = (
            sem(n) for n in ("bias_split", "bias_placed", "squared", "total_ready", "total_copied", "flag_ready"))
        x_loaded, x_first_copied, x_attend_copied, x_second_copied, stored = (
            sem(n) for n in ("x_loaded", "x_first_copied", "x_attend_copied", "x_second_copied", "stored"))
        bn_done, aggregated, spread_ready, rstd_ready, shift_ready, normed = (
            sem(n) for n in ("bn_done", "aggregated", "spread_ready", "rstd_ready", "shift_ready", "normed"))
        twice_ready = sem("twice_ready")
        turned, turned_hi, turned_lo = sem("turned"), sem("turned_hi"), sem("turned_lo")
        gate_ready, up_ready, tanh_ready, silu_ready, hid_ready, hid_hi_ready, hid_lo_ready = (
            sem(n) for n in ("gate_ready", "up_ready", "tanh_ready", "silu_ready", "hid_ready", "hid_hi_ready", "hid_lo_ready"))
        out_ready, out_taken = sem("out_ready"), sem("out_taken")
        qk_ready, qk_taken, rotated, qk_hi_ready, q_lo_ready, k_lo_ready = (
            sem(n) for n in ("qk_ready", "qk_taken", "rotated", "qk_hi_ready", "q_lo_ready", "k_lo_ready"))
        v_ready, v_hi_ready, v_lo_ready = sem("v_ready"), sem("v_hi_ready"), sem("v_lo_ready")
        score_ready, max_ready, bias_ready, exp_ready, inv_ready = (
            sem(n) for n in ("score_ready", "max_ready", "bias_ready", "exp_ready", "inv_ready"))

        gate_blocks = [raw[GATE].rearrange("p (h d) -> p h d", d=D)[:, h, c * P:(c + 1) * P]
                       for c in range(DC) for h in range(CHUNKS)]
        up_blocks = [raw[UP].rearrange("p (h d) -> p h d", d=D)[:, h, c * P:(c + 1) * P]
                     for c in range(DC) for h in range(CHUNKS)]
        down_blocks = [raw[DOWN].rearrange("p (c q h) -> p c h q", c=DC, h=CHUNKS)[:, c, h, :]
                       for h in range(CHUNKS) for c in range(DC)]
        qkv_blocks = {w: [raw_qkv[w].rearrange("p (c d) -> p c d", c=DC)[:, c, dc * P:(dc + 1) * P]
                          for dc in range(DC) for c in range(DC)] for w in (Q, K, V)}
        groups = []
        for n, blocks in ((GATE, gate_blocks), (UP, up_blocks), (DOWN, down_blocks)):
            for g in range(0, len(blocks), 4):
                groups.append((n, blocks[g:g + 4], ffn_hi[:, n, g * P:(g + 4) * P], ffn_lo[:, n, g * P:(g + 4) * P]))
        for w in (Q, K, V):
            groups.append((3 + w, qkv_blocks[w], qkv_hi[:, w, :], qkv_lo[:, w, :]))
        GROUPS, FFN_GROUPS = len(groups), len(gate_blocks) // 4

        norm_source = {"n1": x_in, "n2": x_first, "n3": x_norm3}
        half = {"a": 0, "b": 1}

        def turned_x(parts, name):
            h = half[name[2]]
            return parts[int(name[1])][:, :, h * 2 * P:(h + 1) * 2 * P]

        first = Step(START)

        def chunk_stage(s):
            return FIRST if s < CHUNKS else SECOND

        def run(eng, iteration, start=START + 1, steady_end=STEADY_END):
            for i in range(start, STEADY):
                iteration(Step(i))
            with eng.Fori(0, steady_end - STEADY) as r:
                iteration(Step(STEADY, r))
            for i in range(steady_end, END):
                iteration(Step(i))

        block = ctx.enter_context(nc.Block())

        @block.sync
        def _(sp):
            sp.dma_start(raw[GATE].bitcast(I32), w_gate.rearrange("(p h) d -> p (h d)", h=CHUNKS)).then_inc(w_loaded[GATE], 16)
            sp.dma_start(x_in[:], x[0].rearrange("(p t) d -> p t d", t=TILES)).then_inc(x_loaded, 16)
            sp.dma_start(raw[DOWN].bitcast(I32).rearrange("p (c n) -> p c n", c=DC),
                         w_down.rearrange("(c p) n -> p c n", p=P)).then_inc(w_loaded[DOWN], 16)
            for w, weight in ((Q, wq), (K, wk)):
                sp.dma_start(raw_qkv[w], weight.rearrange("(p c) d -> p (c d)", c=DC)).then_inc(w_loaded[3 + w], 16)
            sp.dma_start(raw_qkv[V].rearrange("p (c d) -> p c d", c=DC),
                          wv.rearrange("(c p) d -> p c d", p=P)).then_inc(w_loaded[3 + V], 16)
            sp.dma_start(rope_sb[:], rope.rearrange("n p t -> p n t")).then_inc(const_loaded, 16)
            for w, bias in ((Q, bq), (K, bk)):
                sp.dma_start(qk_bias[:, w], bias.rearrange("(p c) -> p c", c=DC)).then_inc(const_loaded, 16)
            for row in range(2):
                sp.dma_start(v_bias[row:row + 1, :], bv.rearrange("(a d) -> a d", a=1)).then_inc(const_loaded, 16)
            sp.wait_ge(bias_split, 2)
            sp.dma_start(v_bias_parts[1:2, :].bitcast(F32), v_bias_lo[0:1, :].bitcast(F32)).then_inc(bias_placed, 16)

            def batch(s, stage, later=0):
                n = s.i - LAG[stage] + later
                return n if s.r is None else sp.snap(s.r + n)

            def iteration(s):
                if s.has(SECOND_DOWN):
                    finished = out[batch(s, SECOND_DOWN)].rearrange("(p t) d -> p t d", t=TILES)
                    sp.wait_ge(out_taken, s.after("out", "second3"))
                    sp.dma_start(finished, x_second).then_inc(stored, 16)
                if s.has(SECOND):
                    if s.has(SECOND_DOWN):
                        sp.wait_ge(stored, s.times(SECOND_DOWN, 16, 16))
                    else:
                        sp.wait_ge(normed, s.after("norm", "n3b"))
                    sp.dma_start(x_second, x_norm3).then_inc(x_second_copied, 16)
                if s.has(FIRST):
                    sp.wait_ge(out_taken, s.after("out", "attend3" if s.has(ATTEND) else "first3"))
                    sp.dma_start(x_attend, x_first[:]).then_inc(x_attend_copied, 16)
                if s.has(AHEAD):
                    if s.has(FIRST):
                        sp.wait_ge(x_attend_copied, s.times(FIRST, 16, 16))
                        sp.wait_ge(normed, s.after("norm", "n2b"))
                    else:
                        sp.wait_ge(normed, s.after("norm", "n1b"))
                    sp.dma_start(x_first[:], x_in[:]).then_inc(x_first_copied, 16)
                if active(AHEAD, s.i + 1):
                    coming = x[batch(s, AHEAD, 1)].rearrange("(p t) d -> p t d", t=TILES)
                    sp.wait_ge(x_first_copied, s.times(AHEAD, 16, 16))
                    sp.dma_start(x_in[:], coming).then_inc(x_loaded, 16)

            run(sp, iteration, START, STEADY_END - 1)
            sp.wait_ge(stored, 16 * BATCHES)

        @block.gpsimd
        def _(pool):
            pool.memset(ident[:], 0.0).then_inc(made, 1)
            pool.memset(ones[:], 1.0).then_inc(made, 1)
            pool.memset(minus_half[:], -0.5).then_inc(made, 1)
            pool.wait_ge(made, 1)
            pool.affine_select(out=ident[:], in_=ident[:], compare_op=ALU.not_equal, fill=1.0,
                               base=0, pattern=[[-1, P]], channel_multiplier=1).then_inc(made, 1)

            def inverse_std(s, name):
                h = half[name[2]]
                n = s.before("norm", name)
                pool.wait_ge(spread_ready, (n + 1) * 2)
                nc.gpsimd.tensor_tensor(rstd[:, h], var_eps[:, h], minus_half[:], ALU.pow).then_inc(rstd_ready, 1)
                pool.wait_ge(rstd_ready, n + 1)
                nc.gpsimd.tensor_tensor(shift[:, h], minus_mean[:, h], rstd[:, h], ALU.mult).then_inc(shift_ready, 1)

            def hidden_lo(s, slot):
                n = s.before("chunk", slot)
                f = chunk_stage(slot)
                pool.wait_ge(hid_hi_ready, n + 1)
                nc.gpsimd.tensor_tensor(hid_lo[f][:, slot % CHUNKS], hid[:, slot % 3],
                                        hid_hi[f][:, slot % CHUNKS].bitcast(F32), ALU.subtract).then_inc(hid_lo_ready, 1)

            def rotate(s, w):
                pool.wait_ge(qk_taken, s.times(ATTEND, 2, w + 1))
                nc.gpsimd.tensor_tensor(turned_qk[:, w, 0], turned_qk[:, w, 0], cross[:, 0], ALU.subtract)
                nc.gpsimd.tensor_tensor(turned_qk[:, w, 1], turned_qk[:, w, 1], cross[:, 1], ALU.add).then_inc(rotated, 1)

            def query_lo(s):
                pool.wait_ge(qk_hi_ready, s.times(ATTEND, 2, 1))
                nc.gpsimd.tensor_tensor(qk_lo[:, Q], turned_qk[:, Q], qk_hi[:, Q].bitcast(F32),
                                        ALU.subtract).then_inc(q_lo_ready, 1)

            def iteration(s):
                for slot in range(SLOTS):
                    if s.has(chunk_stage(slot)):
                        hidden_lo(s, slot)
                    for name in s.norms(slot, STATISTICS):
                        inverse_std(s, name)
                    if s.has(ATTEND) and slot == 3:
                        query_lo(s)
                    if s.has(ATTEND) and slot == 2:
                        rotate(s, K)
                    if s.has(ATTEND) and slot == 1:
                        rotate(s, Q)

            pool.wait_ge(made, 4)
            inverse_std(first, "n1a")
            inverse_std(first, "n1b")
            run(pool, iteration)

        @block.scalar
        def _(act):
            act.dma_start(raw[UP].bitcast(I32), w_up.rearrange("(p h) d -> p (h d)", h=CHUNKS)).then_inc(w_loaded[UP], 16)

            def normalise(s, name):
                n = s.before("norm", name)
                h = half[name[2]]
                act.wait_ge(shift_ready, n + 1)
                before = {"n3a": s.start("turn"), "n3b": s.after("turn", "n2b"), "n1a": s.after("turn", "n3a"),
                          "n1b": s.after("turn", "n3b"), "n2a": s.after("turn", "n1a"), "n2b": s.after("turn", "n1b")}[name]
                reuse(act, turned, before)
                for u in range(2):
                    last = nc.scalar.activation(xn[:, h, u], norm_source[name[:2]][:, 2 * h + u], ACT.Identity,
                                                bias=shift[:, h, u:u + 1], scale=rstd[:, h, u:u + 1])
                last.then_inc(normed, 1)

            def norm_hi(s, name):
                act.wait_ge(turned, s.before("turn", name) + 1)
                if name[:2] == "n1":
                    reuse(act, up_ready, s.after("chunk", CHUNKS - 1))
                elif name == "n2a":
                    reuse(act, v_ready, s.times(FIRST, 2, 0))
                elif name == "n3a":
                    reuse(act, up_ready, s.start("chunk"))
                nc.scalar.activation(turned_x(xt_hi, name), turn_ps[:].rearrange("p (c t) -> p c t", c=DC),
                                     ACT.Copy).then_inc(turned_hi, 1)

            def tanh(s, slot):
                act.wait_ge(gate_ready, s.before("chunk", slot) + 1)
                nc.scalar.activation(gated[:, slot % 2], gate_ps[slot % 2][:], ACT.Tanh,
                                     scale=0.5 * WEIGHT_SCALE).then_inc(tanh_ready, 1)

            def hidden_hi(s, slot):
                f = chunk_stage(slot)
                act.wait_ge(hid_ready, s.before("chunk", slot) + 1)
                if slot == 0:
                    reuse(act, out_ready, s.start("out"))
                if slot == CHUNKS:
                    reuse(act, out_ready, s.after("out", "second3"))
                nc.scalar.activation(hid_hi[f][:, slot % CHUNKS], hid[:, slot % 3], ACT.Copy).then_inc(hid_hi_ready, 1)

            def rotated_hi(s, w):
                act.wait_ge(rotated, s.times(ATTEND, 2, w + 1))
                nc.scalar.activation(qk_hi[:, w], turned_qk[:, w], ACT.Copy).then_inc(qk_hi_ready, 1)

            def values_hi(s, pair):
                if pair == 0:
                    reuse(act, out_ready, s.start("out"))
                act.wait_ge(v_ready, s.times(ATTEND, 2, pair + 1))
                nc.scalar.activation(v_hi[:, 2 * pair:2 * pair + 2], att_ps[pair][:].rearrange("p (u d) -> p u d", u=2),
                                     ACT.Copy).then_inc(v_hi_ready, 1)

            def exponent(s, t):
                reuse(act, turned, s.start("turn") if t < 2 else s.after("turn", f"p{t - 2}"))
                act.wait_ge(bias_ready, s.times(ATTEND, TILES, t + 1))
                nc.scalar.activation(prob[:, t % 2], att_ps[t % 2][:], ACT.Exp, bias=exp_bias[:, t:t + 1],
                                     scale=D ** -0.5, accum_out=prob_sum[:, t:t + 1]).then_inc(exp_ready, 1)

            def prob_hi(s, t):
                act.wait_ge(turned, s.before("turn", f"p{t}") + 1)
                reuse(act, out_ready, s.start("out") if t == 0 else s.after("out", f"attend{t - 1}"))
                nc.scalar.activation(pt_hi[:], turn_ps[:].rearrange("p (k q) -> p k q", k=TILES),
                                     ACT.Copy).then_inc(turned_hi, 1)

            def iteration(s):
                attend = s.has(ATTEND)
                for slot in range(SLOTS):
                    if s.has(chunk_stage(slot)):
                        tanh(s, slot)
                    for name in s.norms(slot, APPLY):
                        normalise(s, name)
                    for name in s.norms(slot, TURN):
                        norm_hi(s, name)
                    if s.has(chunk_stage(slot)):
                        hidden_hi(s, slot)
                    if attend and slot == 2:
                        rotated_hi(s, Q)
                    if attend and slot == 4:
                        values_hi(s, 0)
                        values_hi(s, 1)
                    if attend and slot == 4:
                        rotated_hi(s, K)
                    if attend and 7 <= slot < 7 + TILES:
                        prob_hi(s, slot - 7)
                    if attend and 6 <= slot < 6 + TILES:
                        exponent(s, slot - 6)

            def weight_hi(g):
                act.wait_ge(setup_turned, g + 1)
                nc.scalar.activation(groups[g][2], setup_ps[g % len(setup_ps)][:], ACT.Copy).then_inc(setup_hi, 1)

            def lo_square(n, scratch):
                act.wait_ge(setup_lo, (n + 1) * FFN_GROUPS)
                nc.scalar.activation(scratch, ffn_lo[:, n].bitcast(F32), ACT.Square,
                                     accum_out=lo_squares[:, n:n + 1]).then_inc(squared, 1)

            for g in range(2 * FFN_GROUPS):
                weight_hi(g)
            normalise(first, "n1a")
            normalise(first, "n1b")
            norm_hi(first, "n1a")
            lo_square(GATE, raw[GATE])
            for g in range(2 * FFN_GROUPS, 3 * FFN_GROUPS):
                weight_hi(g)
            norm_hi(first, "n1b")
            lo_square(UP, raw[UP])
            lo_square(DOWN, raw[DOWN])
            for g in range(3 * FFN_GROUPS, GROUPS):
                weight_hi(g)
            run(act, iteration)

        @block.vector
        def _(dve):
            def statistics(s, name):
                n = s.before("norm", name)
                h = half[name[2]]
                if name == "n1a":
                    dve.wait_ge(x_loaded, s.times(AHEAD, 16, 16))
                elif name == "n3a":
                    dve.wait_ge(out_taken, s.start("out"))
                elif name in ("n2a", "n2b"):
                    dve.wait_ge(out_taken, s.after("out", "first1" if name == "n2a" else "first3"))
                reuse(dve, normed, n - 1)
                for u in range(2):
                    last = nc.vector.bn_stats(bn[:, h, u], norm_source[name[:2]][:, 2 * h + u])
                last.then_inc(bn_done, 1)
                dve.wait_ge(bn_done, n + 1)
                nc.vector.scalar_tensor_tensor(minus_twice[:, h], bn[:, h, :, 1], -1.0, bn[:, h, :, 4],
                                               ALU.mult, ALU.subtract).then_inc(twice_ready, 1)
                for u in range(2):
                    last = nc.vector.bn_aggr(mean_var[:, h, u], bn[:, h, u])
                last.then_inc(aggregated, 1)
                dve.wait_ge(aggregated, n + 1)
                nc.vector.tensor_scalar(var_eps[:, h], mean_var[:, h, :, 1], EPS, None, ALU.add).then_inc(spread_ready, 1)
                dve.wait_ge(twice_ready, n + 1)
                nc.vector.tensor_scalar(minus_mean[:, h], minus_twice[:, h], 0.5, None, ALU.mult).then_inc(spread_ready, 1)

            def norm_lo(s, name):
                dve.wait_ge(turned_hi, s.before("turn", name) + 1)
                nc.vector.tensor_tensor(turned_x(xt_lo, name), turn_ps[:].rearrange("p (c t) -> p c t", c=DC),
                                        turned_x(xt_hi, name).bitcast(F32), ALU.subtract).then_inc(turned_lo, 1)

            def silu(s, slot):
                n = s.before("chunk", slot)
                dve.wait_ge(tanh_ready, n + 1)
                nc.vector.scalar_tensor_tensor(gated[:, slot % 2], gated[:, slot % 2], 1.0, gate_ps[slot % 2][:],
                                               ALU.add, ALU.mult).then_inc(silu_ready, 1)

            def hidden(s, slot):
                n = s.before("chunk", slot)
                dve.wait_ge(silu_ready, n + 1)
                dve.wait_ge(up_ready, n + 1)
                reuse(dve, hid_lo_ready, n - 2)
                nc.vector.tensor_tensor(hid[:, slot % 3], gated[:, slot % 2], up_ps[slot % 2][:],
                                        ALU.mult).then_inc(hid_ready, 1)

            def rope_products(s, w):
                dve.wait_ge(qk_ready, s.times(ATTEND, 2, w + 1))
                if w == K:
                    dve.wait_ge(rotated, s.times(ATTEND, 2, 1))
                cos, sin = rope_sb[:, 0], rope_sb[:, 1]
                for ps, c, table, product in ((att_ps[0], 0, cos, turned_qk[:, w, 0]), (att_ps[0], 0, sin, turned_qk[:, w, 1]),
                                              (att_ps[1], 1, sin, cross[:, 0]), (att_ps[1], 1, cos, cross[:, 1])):
                    last = nc.vector.scalar_tensor_tensor(product, ps[:], qk_bias[:, w, c:c + 1], table, ALU.add, ALU.mult)
                last.then_inc(qk_taken, 1)

            def key_lo(s):
                dve.wait_ge(qk_hi_ready, s.times(ATTEND, 2, 2))
                nc.vector.tensor_tensor(qk_lo[:, K], turned_qk[:, K], qk_hi[:, K].bitcast(F32),
                                        ALU.subtract).then_inc(k_lo_ready, 1)

            def values_lo(s, pair):
                dve.wait_ge(v_hi_ready, s.times(ATTEND, 2, pair + 1))
                nc.vector.tensor_tensor(v_lo[:, 2 * pair:2 * pair + 2], att_ps[pair][:].rearrange("p (u d) -> p u d", u=2),
                                        v_hi[:, 2 * pair:2 * pair + 2].bitcast(F32), ALU.subtract).then_inc(v_lo_ready, 1)

            def row_max(s, t):
                dve.wait_ge(score_ready, s.times(ATTEND, TILES, t + 1))
                nc.vector.tensor_reduce(minus_max[:, t:t + 1], att_ps[t % 2][:], AX_X, ALU.max,
                                        negate=True).then_inc(max_ready, 1)
                dve.wait_ge(max_ready, s.times(ATTEND, TILES, t + 1))
                nc.vector.tensor_scalar(exp_bias[:, t:t + 1], minus_max[:, t:t + 1], D ** -0.5, None,
                                        ALU.mult).then_inc(bias_ready, 1)

            def prob_lo(s, t):
                dve.wait_ge(turned_hi, s.before("turn", f"p{t}") + 1)
                nc.vector.tensor_tensor(pt_lo[:], turn_ps[:].rearrange("p (k q) -> p k q", k=TILES),
                                        pt_hi[:].bitcast(F32), ALU.subtract).then_inc(turned_lo, 1)
                nc.vector.reciprocal(prob_inv[:, t:t + 1], prob_sum[:, t:t + 1]).then_inc(inv_ready, 1)

            def attended(s, t):
                dve.wait_ge(out_ready, s.before("out", f"attend{t}") + 1)
                dve.wait_ge(inv_ready, s.times(ATTEND, TILES, t + 1))
                if t == 0:
                    dve.wait_ge(x_attend_copied, s.times(ATTEND, 16, 16))
                    reuse(dve, x_second_copied, s.times(ATTEND, 16, 0))
                nc.vector.scalar_tensor_tensor(x_norm3[:, t], out_ps[:, 0:D], prob_inv[:, t:t + 1], x_attend[:, t],
                                               ALU.mult, ALU.add).then_inc(out_taken, 1)

            def fed(s, stage, t, name, source, target):
                dve.wait_ge(out_ready, s.before("out", f"{name}{t}") + 1)
                if t == 0 and stage == FIRST:
                    dve.wait_ge(x_first_copied, s.times(FIRST, 16, 16))
                if t == 0 and stage == SECOND_DOWN:
                    dve.wait_ge(x_second_copied, s.times(SECOND_DOWN, 16, 16))
                nc.vector.scalar_tensor_tensor(target[:, t], out_ps[:, 0:D], 0.25 * WEIGHT_SCALE ** 3, source[:, t],
                                               ALU.mult, ALU.add).then_inc(out_taken, 1)

            def iteration(s):
                attend = s.has(ATTEND)
                for slot in range(SLOTS):
                    if attend and 8 <= slot < 8 + TILES:
                        attended(s, slot - 8)
                    if s.has(chunk_stage(slot)):
                        silu(s, slot)
                    if s.has(chunk_stage(slot)):
                        hidden(s, slot)
                    for name in s.norms(slot, STATISTICS):
                        if name in EARLY:
                            statistics(s, name)
                    for name in s.norms(slot, TURN):
                        norm_lo(s, name)
                    if s.has(SECOND_DOWN) and 2 <= slot < 2 + TILES:
                        fed(s, SECOND_DOWN, slot - 2, "second", x_second, x_second)
                    if s.has(FIRST) and 7 <= slot < 7 + TILES:
                        fed(s, FIRST, slot - 7, "first", x_first, x_first)
                    if attend and 7 <= slot < 7 + TILES:
                        prob_lo(s, slot - 7)
                    if attend and slot == 1:
                        rope_products(s, Q)
                    if attend and slot == 2:
                        rope_products(s, K)
                    if attend and slot == 4:
                        values_lo(s, 0)
                        values_lo(s, 1)
                    if attend and slot == 4:
                        key_lo(s)
                    if attend and 6 <= slot < 6 + TILES:
                        row_max(s, slot - 6)
                    for name in s.norms(slot, STATISTICS):
                        if name not in EARLY:
                            statistics(s, name)

            def cast_weight(n):
                dve.wait_ge(w_loaded[n], 16)
                nc.vector.tensor_copy(raw[n], raw[n].bitcast(I32)).then_inc(cast, 1)

            def weight_lo(g):
                dve.wait_ge(setup_hi, g + 1)
                nc.vector.tensor_tensor(groups[g][3], setup_ps[g % len(setup_ps)][:], groups[g][2].bitcast(F32),
                                        ALU.subtract).then_inc(setup_lo, 1)

            cast_weight(GATE)
            cast_weight(UP)
            statistics(first, "n1a")
            statistics(first, "n1b")
            for g in range(FFN_GROUPS):
                weight_lo(g)
            cast_weight(DOWN)
            for g in range(FFN_GROUPS, 2 * FFN_GROUPS):
                weight_lo(g)
            norm_lo(first, "n1a")
            for g in range(2 * FFN_GROUPS, 3 * FFN_GROUPS):
                weight_lo(g)
            norm_lo(first, "n1b")
            dve.wait_ge(squared, 3)
            nc.vector.tensor_reduce(lo_total[:], lo_squares[:], AX_X, ALU.add).then_inc(total_ready, 1)
            dve.wait_ge(total_copied, 1)
            nc.vector.tensor_scalar(wide_flag[:], turn_ps[0:1, 0:1], 1.0, None, ALU.min).then_inc(flag_ready, 1)
            for g in range(3 * FFN_GROUPS, GROUPS):
                weight_lo(g)
            dve.wait_ge(made, 4)
            nc.vector.tensor_copy(ones_r[:], ones[0:2, :]).then_inc(bias_split, 1)
            dve.wait_ge(const_loaded, 16 * 5)
            nc.vector.tensor_copy(v_bias_parts[0:1, :], v_bias[0:1, :]).then_inc(cast, 1)
            dve.wait_ge(cast, 4)
            nc.vector.tensor_tensor(v_bias_lo[0:1, :], v_bias[0:1, :], v_bias_parts[0:1, :].bitcast(F32),
                                    ALU.subtract).then_inc(bias_split, 1)

            run(dve, iteration)

        @block.tensor
        def _(pe):
            def norm_turn(s, name):
                h = half[name[2]]
                pe.wait_ge(normed, s.start("norm") if name == "n2b" else s.after("norm", name))
                reuse(pe, turned_lo, s.before("turn", name))
                for u in range(2):
                    for c in range(DC):
                        last = nc.tensor.transpose(turn_ps[:, c * 2 * P + u * P:c * 2 * P + (u + 1) * P],
                                                   xn[:, h, u, c * P:(c + 1) * P], ident[:])
                last.then_inc(turned, 1)

            pe.wait_ge(made, 4)
            for g, (weight, blocks, _, _) in enumerate(groups):
                if weight < 3:
                    pe.wait_ge(cast, weight + 1)
                else:
                    pe.wait_ge(w_loaded[weight], 16)
                reuse(pe, setup_lo, g - len(setup_ps) + 1)
                for n, b in enumerate(blocks):
                    last = nc.tensor.transpose(setup_ps[g % len(setup_ps)][:, n * P:(n + 1) * P], b, ident[:])
                last.then_inc(setup_turned, 1)
                if g == 2 * FFN_GROUPS - 1:
                    norm_turn(first, "n1a")
                if g == 3 * FFN_GROUPS - 1:
                    norm_turn(first, "n1b")
            pe.wait_ge(total_ready, 1)
            nc.tensor.matmul(turn_ps[0:1, 0:1], lo_total[:], ones[:, 0:1], start=True, stop=True).then_inc(total_copied, 1)
            pe.wait_ge(flag_ready, 1)
            wide = pe.value_load(wide_flag[0:1, 0:1], min_val=0, max_val=1)

            def products(out, terms):
                for n, (lhs_t, rhs) in enumerate(terms):
                    last = nc.tensor.matmul(out, lhs_t, rhs, start=(n == 0), stop=(n == len(terms) - 1))
                return last

            def program(ffn_passes):
                def chunk(s, slot, w, ps, ready):
                    n = s.before("chunk", slot)
                    h = slot % CHUNKS
                    norm = 1 if slot < CHUNKS else 3
                    if w == GATE and h == 0:
                        pe.wait_ge(turned_lo, s.start("turn") if norm == 1 else s.after("turn", "n3b"))
                    if w == GATE:
                        reuse(pe, hid_ready, n - 1)
                    terms = []
                    for c in range(DC):
                        hi, lo = (part[:, w, c * HIDDEN + h * P:c * HIDDEN + (h + 1) * P] for part in (ffn_hi, ffn_lo))
                        terms += [(hi, xt_hi[norm][:, c]), (hi, xt_lo[norm][:, c]), (lo, xt_hi[norm][:, c])][:ffn_passes]
                    products(ps[slot % 2][:], terms).then_inc(ready, 1)

                def down(s, f, name, t, chunks_done):
                    if t == 0:
                        pe.wait_ge(hid_lo_ready, chunks_done)
                    if s.i == START + 1:
                        pe.wait_ge(setup_lo, GROUPS)
                    reuse(pe, out_taken, s.before("out", f"{name}{t}"))
                    terms = []
                    for h in range(CHUNKS):
                        hi, lo = (part[f][:, h, t * P:(t + 1) * P] for part in (hid_hi, hid_lo))
                        w_hi, w_lo = (part[:, DOWN, h * D:(h + 1) * D] for part in (ffn_hi, ffn_lo))
                        terms += [(hi, w_hi), (lo, w_hi), (hi, w_lo)][:ffn_passes]
                    products(out_ps[:, 0:D], terms).then_inc(out_ready, 1)

                def project(s, w):
                    if w == Q:
                        pe.wait_ge(turned_lo, s.after("turn", "n2b"))
                        reuse(pe, exp_ready, s.times(ATTEND, TILES, 0))
                    else:
                        pe.wait_ge(qk_taken, s.times(ATTEND, 2, 1))
                    for c in range(DC):
                        terms = []
                        for dc in range(DC):
                            hi, lo = (part[:, w, (dc * DC + c) * P:(dc * DC + c + 1) * P] for part in (qkv_hi, qkv_lo))
                            terms += [(hi, xt_hi[2][:, dc]), (hi, xt_lo[2][:, dc]), (lo, xt_hi[2][:, dc])]
                        last = products(att_ps[c][:], terms)
                    last.then_inc(qk_ready, 1)

                def values(s, pair):
                    if pair == 0:
                        pe.wait_ge(bias_split, 2)
                        pe.wait_ge(bias_placed, 16)
                    pe.wait_ge(qk_taken, s.times(ATTEND, 2, 2))
                    for u in range(2):
                        at = (2 * pair + u) * P
                        terms = [(ones_r[:], v_bias_parts[:])]
                        for dc in range(DC):
                            hi, lo = (part[:, V, dc * D:(dc + 1) * D] for part in (qkv_hi, qkv_lo))
                            x_hi, x_lo = xt_hi[2][:, dc, at:at + P], xt_lo[2][:, dc, at:at + P]
                            terms += [(x_hi, hi), (x_hi, lo), (x_lo, hi)]
                        last = products(att_ps[pair][:, u * D:(u + 1) * D], terms)
                    last.then_inc(v_ready, 1)

                def scores(s, t):
                    if t == 0:
                        pe.wait_ge(q_lo_ready, s.times(ATTEND, 1, 1))
                        pe.wait_ge(k_lo_ready, s.times(ATTEND, 1, 1))
                    if t < 2:
                        pe.wait_ge(v_lo_ready, s.times(ATTEND, 2, t + 1))
                    else:
                        pe.wait_ge(exp_ready, s.times(ATTEND, TILES, t - 1))
                    terms = []
                    for c in range(DC):
                        q_hi, q_lo = (part[:, Q, c, t * P:(t + 1) * P] for part in (qk_hi, qk_lo))
                        terms += [(q_hi, qk_hi[:, K, c]), (q_hi, qk_lo[:, K, c]), (q_lo, qk_hi[:, K, c])]
                    products(att_ps[t % 2][:], terms).then_inc(score_ready, 1)

                def prob_turn(s, t):
                    pe.wait_ge(exp_ready, s.times(ATTEND, TILES, t + 1))
                    reuse(pe, turned_lo, s.before("turn", f"p{t}"))
                    for k in range(TILES):
                        last = nc.tensor.transpose(turn_ps[:, k * P:(k + 1) * P], prob[:, t % 2, k * P:(k + 1) * P], ident[:])
                    last.then_inc(turned, 1)

                def weigh(s, t):
                    pe.wait_ge(turned_lo, s.after("turn", f"p{t}"))
                    reuse(pe, out_taken, s.before("out", f"attend{t}"))
                    terms = []
                    for k in range(TILES):
                        terms += [(pt_hi[:, k], v_hi[:, k]), (pt_hi[:, k], v_lo[:, k]), (pt_lo[:, k], v_hi[:, k])]
                    products(out_ps[:, 0:D], terms).then_inc(out_ready, 1)

                def iteration(s):
                    attend = s.has(ATTEND)
                    for slot in range(SLOTS):
                        if s.has(chunk_stage(slot)):
                            chunk(s, slot, GATE, gate_ps, gate_ready)
                        if attend and 8 <= slot < 8 + TILES:
                            weigh(s, slot - 8)
                        if s.has(chunk_stage(slot)):
                            chunk(s, slot, UP, up_ps, up_ready)
                        for name in s.norms(slot, TURN):
                            norm_turn(s, name)
                        if s.has(SECOND_DOWN) and 2 <= slot < 2 + TILES:
                            down(s, SECOND, "second", slot - 2, s.start("chunk"))
                        if s.has(FIRST) and 7 <= slot < 7 + TILES:
                            down(s, FIRST, "first", slot - 7, s.after("chunk", CHUNKS - 1))
                        if attend and slot == 2:
                            project(s, K)
                        if attend and 7 <= slot < 7 + TILES:
                            prob_turn(s, slot - 7)
                        if attend and slot == 1:
                            project(s, Q)
                        if attend and 6 <= slot < 6 + TILES:
                            scores(s, slot - 6)
                        if attend and slot == 4:
                            values(s, 0)
                            values(s, 1)

                run(pe, iteration)

            with pe.If(wide > 0):
                program(3)
            with pe.Else():
                program(2)


def rope_tables():
    inv_freq = (1.0 / np.float32(THETA) ** (np.arange(0, D, 2, dtype=np.float32) / np.float32(D))).astype(np.float32)
    token = np.arange(TOKENS).reshape(P, TILES).T.reshape(-1).astype(np.float32)
    angle = inv_freq[:, None] * token[None, :]
    return np.stack([np.cos(angle), np.sin(angle)]).astype(np.float32)


INPUTS = ["L0_attn_x", "L0_attn_wq_w", "L0_attn_wq_b", "L0_attn_wk_w", "L0_attn_wk_b", "L0_attn_wv_w",
          "L0_attn_wv_b", "L0_ffn_w_gate", "L0_ffn_w_up", "L0_ffn_w_down"]


def kernel(**inputs):
    import concourse.bacc as bacc
    from concourse.bass_utils import run_bass_kernel_spmd

    nc = bacc.Bacc("TRN2", target_bir_lowering=False, num_devices=1)
    arrays = {name: np.ascontiguousarray(inputs[name]) for name in INPUTS}
    arrays["rope"] = rope_tables()
    args = [nc.dram_tensor(f"in_{name}", a.shape, mybir.dt.from_np(a.dtype), kind="ExternalInput").ap()
            for name, a in arrays.items()]
    out = nc.dram_tensor("out", (BATCHES, TOKENS, D), F32, kind="ExternalOutput").ap()
    build(nc, *args, out)
    result = run_bass_kernel_spmd(nc, [{f"in_{name}": a for name, a in arrays.items()}], core_ids=[0])
    return result.results[0]["out"]
```

```python
from contextlib import ExitStack

import numpy as np

import concourse.bass as bass
from concourse import mybir

F32 = mybir.dt.float32
F32R = mybir.dt.float32r
I32 = mybir.dt.int32
ALU = mybir.AluOpType
ACT = mybir.ActivationFunctionType
AX_X = mybir.AxisListType.X

P = 128
BATCHES, TOKENS, D = 16, 512, 256
HIDDEN = 768
TILES = TOKENS // P
DC = D // P
CHUNKS = HIDDEN // P
SLOTS = 2 * CHUNKS
EPS = 1e-5
THETA = 10000.0
WEIGHT_SCALE = 1.0 / 127.0
GATE, UP, DOWN = range(3)
Q, K, V = range(3)

FIRST, ATTEND, SECOND, SECOND_DOWN, AHEAD = "first", "attend", "second", "second_down", "ahead"
LAG = {AHEAD: -1, FIRST: 0, ATTEND: 1, SECOND: 2, SECOND_DOWN: 3}
START, STEADY, STEADY_END, END = -1, 4, 15, BATCHES + 3

ORDER = {
    "chunk": [(s, FIRST if s < CHUNKS else SECOND) for s in range(SLOTS)],
    "norm": [("n3a", SECOND), ("n3b", SECOND), ("n1a", AHEAD), ("n1b", AHEAD), ("n2a", FIRST), ("n2b", FIRST)],
    "turn": [("n2b", ATTEND), ("n3a", SECOND), ("n3b", SECOND), ("n1a", AHEAD),
             ("p0", ATTEND), ("n1b", AHEAD), ("p1", ATTEND),
             ("p2", ATTEND), ("n2a", FIRST), ("p3", ATTEND)],
    "out": [("second0", SECOND_DOWN), ("second1", SECOND_DOWN), ("second2", SECOND_DOWN), ("second3", SECOND_DOWN),
            ("first0", FIRST), ("attend0", ATTEND), ("first1", FIRST), ("attend1", ATTEND),
            ("first2", FIRST), ("attend2", ATTEND), ("first3", FIRST), ("attend3", ATTEND)],
}


STATISTICS, APPLY, TURN = range(3)
NORM_SLOTS = {"n3a": (0, 1, 3), "n3b": (2, 3, 4), "n1a": (3, 5, 6), "n1b": (5, 7, 8),
              "n2a": (8, 9, 10), "n2b": (10, 11, 12)}
EARLY = ('n3b',)


def active(stage, i):
    return 0 <= i - LAG[stage] < BATCHES


class Step:

    def __init__(self, i, r=None):
        self.i, self.r = i, r

    def has(self, stage):
        return active(stage, self.i)

    def start(self, kind):
        n = sum(active(stage, j) for j in range(START, self.i) for _, stage in ORDER[kind])
        return n if self.r is None else self.r * len(ORDER[kind]) + n

    def before(self, kind, use):
        names = [name for name, _ in ORDER[kind]]
        return self.start(kind) + sum(active(stage, self.i) for _, stage in ORDER[kind][:names.index(use)])

    def after(self, kind, use):
        stage = dict(ORDER[kind])[use]
        return self.before(kind, use) + active(stage, self.i)

    def norms(self, slot, step):
        for name, slots in NORM_SLOTS.items():
            if slots[step] % SLOTS == slot:
                stage = dict(ORDER["norm"])[name] if slots[step] < SLOTS else dict(ORDER["turn"])[name]
                if self.has(stage):
                    yield name

    def times(self, stage, per, k):
        n = per * (self.i - LAG[stage]) + k
        return n if self.r is None else self.r * per + n


def reuse(eng, sem, value):
    if not isinstance(value, int) or value > 0:
        eng.wait_ge(sem, value)


def build(nc, x, wq, bq, wk, bk, wv, bv, w_gate, w_up, w_down, rope, out):
    with ExitStack() as ctx:
        def sb(name, shape, dt=F32):
            return ctx.enter_context(nc.sbuf_tensor(name, shape, dt))

        def bank(name):
            return ctx.enter_context(nc.psum_tensor(name, [P, 512], F32))

        def sem(name):
            return ctx.enter_context(nc.semaphore(name))

        ffn_hi, ffn_lo = sb("ffn_hi", [P, 3, DC * HIDDEN], F32R), sb("ffn_lo", [P, 3, DC * HIDDEN], F32R)
        qkv_hi, qkv_lo = sb("qkv_hi", [P, 3, DC * D], F32R), sb("qkv_lo", [P, 3, DC * D], F32R)
        rope_sb = sb("rope_sb", [P, 2, TOKENS])
        ident = sb("ident", [P, P])
        ones = sb("ones", [P, P])
        qk_bias = sb("qk_bias", [P, 2, DC])
        v_bias = sb("v_bias", [P, D])
        minus_half = sb("minus_half", [P, 2])
        lo_squares = sb("lo_squares", [P, 3])
        lo_total = sb("lo_total", [P, 1])
        wide_flag = sb("wide_flag", [1, 1], I32)
        x_in = sb("x_in", [P, TILES, D])
        x_first = sb("x_first", [P, TILES, D])
        mid = sb("mid", [P, 3, TILES, D])
        x_attend, x_norm3, x_second = (mid[:, n] for n in range(3))
        xn = sb("xn", [P, 2, 2, D])
        bn = sb("bn", [P, 2, 2, 6])
        mean_var = sb("mean_var", [P, 2, 2, 2])
        var_eps, minus_mean = sb("var_eps", [P, 2, 2]), sb("minus_mean", [P, 2, 2])
        minus_twice = sb("minus_twice", [P, 2, 2])
        rstd, shift = sb("rstd", [P, 2, 2]), sb("shift", [P, 2, 2])
        xt_hi = {n: sb(f"xt_hi{n}", [P, DC, TOKENS], F32R) for n in (1, 2, 3)}
        xt_lo = {n: sb(f"xt_lo{n}", [P, DC, TOKENS], F32R) for n in (1, 2, 3)}
        gated = sb("gated", [P, 2, TOKENS])
        hid = sb("hid", [P, 3, TOKENS])
        hid_hi = {f: sb(f"hid_hi_{f}", [P, CHUNKS, TOKENS], F32R) for f in (FIRST, SECOND)}
        hid_lo = {f: sb(f"hid_lo_{f}", [P, CHUNKS, TOKENS], F32R) for f in (FIRST, SECOND)}
        turned_qk = sb("turned_qk", [P, 2, DC, TOKENS])
        cross = sb("cross", [P, DC, TOKENS])
        qk_hi, qk_lo = sb("qk_hi", [P, 2, DC, TOKENS], F32R), sb("qk_lo", [P, 2, DC, TOKENS], F32R)
        v_hi, v_lo = sb("v_hi", [P, TILES, D], F32R), sb("v_lo", [P, TILES, D], F32R)
        minus_max, exp_bias = sb("minus_max", [P, TILES]), sb("exp_bias", [P, TILES])
        prob_sum, prob_inv = sb("prob_sum", [P, TILES]), sb("prob_inv", [P, TILES])
        prob = sb("prob", [P, 2, TOKENS])
        pt_hi, pt_lo = sb("pt_hi", [P, TILES, P], F32R), sb("pt_lo", [P, TILES, P], F32R)

        raw = {
            GATE: mid[:].rearrange("p n t d -> p (n t d)")[:, 0:CHUNKS * D],
            UP: mid[:].rearrange("p n t d -> p (n t d)")[:, CHUNKS * D:2 * CHUNKS * D],
            DOWN: turned_qk[:].rearrange("p n c t -> p (n c t)")[:, 0:DC * HIDDEN],
        }
        raw_qkv = {
            Q: cross[:].rearrange("p c t -> p (c t)")[:, 0:DC * D],
            K: cross[:].rearrange("p c t -> p (c t)")[:, DC * D:2 * DC * D],
            V: turned_qk[:].rearrange("p n c t -> p (n c t)")[:, DC * HIDDEN:DC * HIDDEN + DC * D],
        }

        gate_ps, up_ps = [bank("gate_ps0"), bank("gate_ps1")], [bank("up_ps0"), bank("up_ps1")]
        att_ps = [bank("att_ps0"), bank("att_ps1")]
        turn_ps, out_ps = bank("turn_ps"), bank("out_ps")
        setup_ps = [*gate_ps, out_ps, *att_ps, *up_ps]

        w_loaded = [sem(f"w_loaded{n}") for n in range(6)]
        const_loaded, made, cast, setup_turned, setup_hi, setup_lo = (
            sem(n) for n in ("const_loaded", "made", "cast", "setup_turned", "setup_hi", "setup_lo"))
        squared, total_ready, total_copied, flag_ready, v_bias_added = (
            sem(n) for n in ("squared", "total_ready", "total_copied", "flag_ready", "v_bias_added"))
        x_loaded, x_first_copied, x_attend_copied, x_second_copied, stored = (
            sem(n) for n in ("x_loaded", "x_first_copied", "x_attend_copied", "x_second_copied", "stored"))
        bn_done, aggregated, spread_ready, rstd_ready, shift_ready, normed = (
            sem(n) for n in ("bn_done", "aggregated", "spread_ready", "rstd_ready", "shift_ready", "normed"))
        twice_ready, first_tile_normed = sem("twice_ready"), sem("first_tile_normed")
        turned, turned_hi, turned_lo = sem("turned"), sem("turned_hi"), sem("turned_lo")
        gate_ready, up_ready, tanh_ready, silu_ready, hid_ready, hid_hi_ready, hid_lo_ready = (
            sem(n) for n in ("gate_ready", "up_ready", "tanh_ready", "silu_ready", "hid_ready", "hid_hi_ready", "hid_lo_ready"))
        out_ready, out_taken = sem("out_ready"), sem("out_taken")
        qk_ready, qk_taken, rotated, qk_hi_ready, q_lo_ready, k_lo_ready = (
            sem(n) for n in ("qk_ready", "qk_taken", "rotated", "qk_hi_ready", "q_lo_ready", "k_lo_ready"))
        v_ready, v_hi_ready, v_lo_ready = sem("v_ready"), sem("v_hi_ready"), sem("v_lo_ready")
        score_ready, max_ready, bias_ready, exp_ready, inv_ready = (
            sem(n) for n in ("score_ready", "max_ready", "bias_ready", "exp_ready", "inv_ready"))

        gate_blocks = [raw[GATE].rearrange("p (h d) -> p h d", d=D)[:, h, c * P:(c + 1) * P]
                       for c in range(DC) for h in range(CHUNKS)]
        up_blocks = [raw[UP].rearrange("p (h d) -> p h d", d=D)[:, h, c * P:(c + 1) * P]
                     for c in range(DC) for h in range(CHUNKS)]
        down_blocks = [raw[DOWN].rearrange("p (c q h) -> p c h q", c=DC, h=CHUNKS)[:, c, h, :]
                       for h in range(CHUNKS) for c in range(DC)]
        qkv_blocks = {w: [raw_qkv[w].rearrange("p (c d) -> p c d", c=DC)[:, c, dc * P:(dc + 1) * P]
                          for dc in range(DC) for c in range(DC)] for w in (Q, K, V)}
        groups = []
        for n, blocks in ((GATE, gate_blocks), (UP, up_blocks), (DOWN, down_blocks)):
            for g in range(0, len(blocks), 4):
                groups.append((n, blocks[g:g + 4], ffn_hi[:, n, g * P:(g + 4) * P], ffn_lo[:, n, g * P:(g + 4) * P]))
        for w in (Q, K, V):
            groups.append((3 + w, qkv_blocks[w], qkv_hi[:, w, :], qkv_lo[:, w, :]))
        GROUPS, FFN_GROUPS = len(groups), len(gate_blocks) // 4

        norm_source = {"n1": x_in, "n2": x_first, "n3": x_norm3}
        half = {"a": 0, "b": 1}

        def turned_x(parts, name):
            h = half[name[2]]
            return parts[int(name[1])][:, :, h * 2 * P:(h + 1) * 2 * P]

        first = Step(START)

        def chunk_stage(s):
            return FIRST if s < CHUNKS else SECOND

        def run(eng, iteration, start=START + 1, steady_end=STEADY_END):
            for i in range(start, STEADY):
                iteration(Step(i))
            with eng.Fori(0, steady_end - STEADY) as r:
                iteration(Step(STEADY, r))
            for i in range(steady_end, END):
                iteration(Step(i))

        def down_bank(s, t):
            return turn_ps if s.i == END - 1 and t % 2 == 1 else out_ps

        block = ctx.enter_context(nc.Block())

        @block.sync
        def _(sp):
            sp.dma_start(raw[GATE].bitcast(I32), w_gate.rearrange("(p h) d -> p (h d)", h=CHUNKS)).then_inc(w_loaded[GATE], 16)
            sp.dma_start(x_in[:], x[0].rearrange("(p t) d -> p t d", t=TILES)).then_inc(x_loaded, 16)
            sp.dma_start(raw[DOWN].bitcast(I32).rearrange("p (c n) -> p c n", c=DC),
                         w_down.rearrange("(c p) n -> p c n", p=P)).then_inc(w_loaded[DOWN], 16)
            for w, weight in ((Q, wq), (K, wk)):
                sp.dma_start(raw_qkv[w], weight.rearrange("(p c) d -> p (c d)", c=DC)).then_inc(w_loaded[3 + w], 16)
            sp.dma_start(raw_qkv[V].rearrange("p (c d) -> p c d", c=DC),
                          wv.rearrange("(c p) d -> p c d", p=P)).then_inc(w_loaded[3 + V], 16)
            sp.dma_start(rope_sb[:], rope.rearrange("n p t -> p n t")).then_inc(const_loaded, 16)
            for w, bias in ((Q, bq), (K, bk)):
                sp.dma_start(qk_bias[:, w], bias.rearrange("(p c) -> p c", c=DC)).then_inc(const_loaded, 16)
            sp.dma_start(v_bias[:], bv.partition_broadcast(P)).then_inc(const_loaded, 16)

            def batch(s, stage, later=0):
                n = s.i - LAG[stage] + later
                return n if s.r is None else sp.snap(s.r + n)

            def iteration(s):
                if s.has(SECOND_DOWN):
                    finished = out[batch(s, SECOND_DOWN)].rearrange("(p t) d -> p t d", t=TILES)
                    tiles = range(TILES) if s.i == END - 1 else range(TILES - 1, TILES)
                    for t in tiles:
                        part = slice(t, t + 1) if s.i == END - 1 else slice(0, TILES)
                        sp.wait_ge(out_taken, s.after("out", f"second{t}"))
                        sp.dma_start(finished[:, part], x_second[:, part]).then_inc(stored, 16)
                if s.has(SECOND):
                    if s.has(SECOND_DOWN):
                        sp.wait_ge(stored, s.times(SECOND_DOWN, 16, 16))
                    else:
                        sp.wait_ge(normed, s.after("norm", "n3b"))
                    sp.dma_start(x_second, x_norm3).then_inc(x_second_copied, 16)
                if s.has(FIRST):
                    sp.wait_ge(out_taken, s.after("out", "attend3" if s.has(ATTEND) else "first3"))
                    sp.dma_start(x_attend, x_first[:]).then_inc(x_attend_copied, 16)
                if s.has(AHEAD):
                    if s.has(FIRST):
                        sp.wait_ge(x_attend_copied, s.times(FIRST, 16, 16))
                        sp.wait_ge(normed, s.after("norm", "n2b"))
                    else:
                        sp.wait_ge(normed, s.after("norm", "n1b"))
                    sp.dma_start(x_first[:], x_in[:]).then_inc(x_first_copied, 16)
                if active(AHEAD, s.i + 1):
                    coming = x[batch(s, AHEAD, 1)].rearrange("(p t) d -> p t d", t=TILES)
                    sp.wait_ge(x_first_copied, s.times(AHEAD, 16, 16))
                    sp.dma_start(x_in[:], coming).then_inc(x_loaded, 16)

            run(sp, iteration, START, STEADY_END - 1)
            sp.wait_ge(stored, 16 * (BATCHES - 1 + TILES))

        @block.gpsimd
        def _(pool):
            pool.memset(ident[:], 0.0).then_inc(made, 1)
            pool.memset(ones[:], 1.0).then_inc(made, 1)
            pool.memset(minus_half[:], -0.5).then_inc(made, 1)
            pool.wait_ge(made, 1)
            pool.affine_select(out=ident[:], in_=ident[:], compare_op=ALU.not_equal, fill=1.0,
                               base=0, pattern=[[-1, P]], channel_multiplier=1).then_inc(made, 1)

            def inverse_std(s, name):
                h = half[name[2]]
                n = s.before("norm", name)
                pool.wait_ge(spread_ready, (n + 1) * 2)
                nc.gpsimd.tensor_tensor(rstd[:, h], var_eps[:, h], minus_half[:], ALU.pow).then_inc(rstd_ready, 1)
                pool.wait_ge(rstd_ready, n + 1)
                nc.gpsimd.tensor_tensor(shift[:, h], minus_mean[:, h], rstd[:, h], ALU.mult).then_inc(shift_ready, 1)

            def hidden_lo(s, slot):
                n = s.before("chunk", slot)
                f = chunk_stage(slot)
                pool.wait_ge(hid_hi_ready, n + 1)
                nc.gpsimd.tensor_tensor(hid_lo[f][:, slot % CHUNKS], hid[:, slot % 3],
                                        hid_hi[f][:, slot % CHUNKS].bitcast(F32), ALU.subtract).then_inc(hid_lo_ready, 1)

            def rotate(s, w):
                pool.wait_ge(qk_taken, s.times(ATTEND, 4, 2 * w + 2))
                nc.gpsimd.tensor_tensor(turned_qk[:, w, 0], turned_qk[:, w, 0], cross[:, 0], ALU.subtract)
                nc.gpsimd.tensor_tensor(turned_qk[:, w, 1], turned_qk[:, w, 1], cross[:, 1], ALU.add).then_inc(rotated, 1)

            def query_lo(s):
                pool.wait_ge(qk_hi_ready, s.times(ATTEND, 2, 1))
                nc.gpsimd.tensor_tensor(qk_lo[:, Q], turned_qk[:, Q], qk_hi[:, Q].bitcast(F32),
                                        ALU.subtract).then_inc(q_lo_ready, 1)

            def add_value_bias(s):
                pool.wait_ge(const_loaded, 16 * 4)
                pool.wait_ge(x_attend_copied, s.times(ATTEND, 16, 16))
                for t in range(TILES):
                    last = nc.gpsimd.tensor_tensor(x_attend[:, t], x_attend[:, t], v_bias[:], ALU.add)
                last.then_inc(v_bias_added, 1)

            def iteration(s):
                for slot in range(SLOTS):
                    if slot > 0 and s.has(chunk_stage(slot - 1)):
                        hidden_lo(s, slot - 1)
                    for name in s.norms(slot, STATISTICS):
                        inverse_std(s, name)
                    if s.has(ATTEND) and slot == 1:
                        rotate(s, Q)
                    if s.has(ATTEND) and slot == 6:
                        add_value_bias(s)
                    if s.has(ATTEND) and slot == 4:
                        query_lo(s)
                    if s.has(ATTEND) and slot == 2:
                        rotate(s, K)
                    if slot == SLOTS - 1 and s.has(SECOND):
                        hidden_lo(s, slot)

            pool.wait_ge(made, 4)
            inverse_std(first, "n1a")
            inverse_std(first, "n1b")
            run(pool, iteration)

        @block.scalar
        def _(act):
            act.dma_start(raw[UP].bitcast(I32), w_up.rearrange("(p h) d -> p (h d)", h=CHUNKS)).then_inc(w_loaded[UP], 16)

            def normalise(s, name):
                n = s.before("norm", name)
                h = half[name[2]]
                act.wait_ge(shift_ready, n + 1)
                before = {"n3a": s.start("turn"), "n3b": s.after("turn", "n2b"), "n1a": s.after("turn", "n3a"),
                          "n1b": s.after("turn", "n3b"), "n2a": s.after("turn", "n1a"), "n2b": s.after("turn", "n1b")}[name]
                reuse(act, turned, before)
                for u in range(2):
                    nc.scalar.activation(xn[:, h, u], norm_source[name[:2]][:, 2 * h + u], ACT.Identity,
                                         bias=shift[:, h, u:u + 1],
                                         scale=rstd[:, h, u:u + 1]).then_inc((first_tile_normed, normed)[u], 1)

            def norm_hi(s, name):
                act.wait_ge(turned, s.before("turn", name) + 1)
                if name[:2] == "n1":
                    reuse(act, up_ready, s.after("chunk", CHUNKS - 1))
                elif name == "n2a":
                    reuse(act, v_ready, s.times(FIRST, 2, 0))
                elif name == "n3a":
                    reuse(act, up_ready, s.start("chunk"))
                nc.scalar.activation(turned_x(xt_hi, name), turn_ps[:].rearrange("p (c t) -> p c t", c=DC),
                                     ACT.Copy).then_inc(turned_hi, 1)

            def tanh(s, slot):
                act.wait_ge(gate_ready, s.before("chunk", slot) + 1)
                reuse(act, hid_ready, s.before("chunk", slot) - 1)
                nc.scalar.activation(gated[:, slot % 2], gate_ps[slot % 2][:], ACT.Tanh,
                                     scale=0.5 * WEIGHT_SCALE).then_inc(tanh_ready, 1)

            def hidden_hi(s, slot):
                f = chunk_stage(slot)
                act.wait_ge(hid_ready, s.before("chunk", slot) + 1)
                if slot == 0:
                    reuse(act, out_ready, s.start("out"))
                if slot == CHUNKS:
                    reuse(act, out_ready, s.after("out", "second3"))
                nc.scalar.activation(hid_hi[f][:, slot % CHUNKS], hid[:, slot % 3], ACT.Copy).then_inc(hid_hi_ready, 1)

            def rotated_hi(s, w):
                act.wait_ge(rotated, s.times(ATTEND, 2, w + 1))
                nc.scalar.activation(qk_hi[:, w], turned_qk[:, w], ACT.Copy).then_inc(qk_hi_ready, 1)

            def values_hi(s, pair):
                if pair == 0:
                    reuse(act, out_ready, s.start("out"))
                act.wait_ge(v_ready, s.times(ATTEND, 2, pair + 1))
                nc.scalar.activation(v_hi[:, 2 * pair:2 * pair + 2], att_ps[pair][:].rearrange("p (u d) -> p u d", u=2),
                                     ACT.Copy).then_inc(v_hi_ready, 1)

            def exponent(s, t):
                reuse(act, turned, s.start("turn") if t < 2 else s.after("turn", f"p{t - 2}"))
                act.wait_ge(bias_ready, s.times(ATTEND, TILES, t + 1))
                nc.scalar.activation(prob[:, t % 2], att_ps[t % 2][:], ACT.Exp, bias=exp_bias[:, t:t + 1],
                                     scale=D ** -0.5, accum_out=prob_sum[:, t:t + 1]).then_inc(exp_ready, 1)

            def prob_hi(s, t):
                act.wait_ge(turned, s.before("turn", f"p{t}") + 1)
                reuse(act, out_ready, s.start("out") if t == 0 else s.after("out", f"attend{t - 1}"))
                nc.scalar.activation(pt_hi[:], turn_ps[:].rearrange("p (k q) -> p k q", k=TILES),
                                     ACT.Copy).then_inc(turned_hi, 1)

            def iteration(s):
                attend = s.has(ATTEND)
                for slot in range(SLOTS):
                    if s.has(chunk_stage(slot)):
                        tanh(s, slot)
                    if slot > 0 and s.has(chunk_stage(slot - 1)):
                        hidden_hi(s, slot - 1)
                    for name in s.norms(slot, TURN):
                        norm_hi(s, name)
                    if attend and slot == 4:
                        rotated_hi(s, K)
                    if attend and 7 <= slot < 7 + TILES:
                        prob_hi(s, slot - 7)
                    for name in s.norms(slot, APPLY):
                        normalise(s, name)
                    if attend and slot == 4:
                        values_hi(s, 0)
                        values_hi(s, 1)
                    if attend and 6 <= slot < 6 + TILES:
                        exponent(s, slot - 6)
                    if attend and slot == 3:
                        rotated_hi(s, Q)
                    if slot == SLOTS - 1 and s.has(SECOND):
                        hidden_hi(s, slot)

            def weight_hi(g):
                act.wait_ge(setup_turned, g + 1)
                nc.scalar.activation(groups[g][2], setup_ps[g % len(setup_ps)][:], ACT.Copy).then_inc(setup_hi, 1)

            def lo_square(n, scratch):
                act.wait_ge(setup_lo, (n + 1) * FFN_GROUPS)
                nc.scalar.activation(scratch, ffn_lo[:, n].bitcast(F32), ACT.Square,
                                     accum_out=lo_squares[:, n:n + 1]).then_inc(squared, 1)

            for g in range(2 * FFN_GROUPS):
                weight_hi(g)
            normalise(first, "n1a")
            normalise(first, "n1b")
            norm_hi(first, "n1a")
            lo_square(GATE, raw[GATE])
            weight_hi(2 * FFN_GROUPS)
            lo_square(UP, raw[UP])
            for g in range(2 * FFN_GROUPS + 1, 3 * FFN_GROUPS):
                weight_hi(g)
            norm_hi(first, "n1b")
            lo_square(DOWN, raw[DOWN])
            for g in range(3 * FFN_GROUPS, GROUPS):
                weight_hi(g)
            run(act, iteration)

        @block.vector
        def _(dve):
            def statistics(s, name):
                n = s.before("norm", name)
                h = half[name[2]]
                if name == "n1a":
                    dve.wait_ge(x_loaded, s.times(AHEAD, 16, 16))
                elif name == "n3a":
                    dve.wait_ge(out_taken, s.start("out"))
                elif name in ("n2a", "n2b"):
                    dve.wait_ge(out_taken, s.after("out", "first1" if name == "n2a" else "first3"))
                reuse(dve, normed, n - 1)
                for u in range(2):
                    last = nc.vector.bn_stats(bn[:, h, u], norm_source[name[:2]][:, 2 * h + u])
                last.then_inc(bn_done, 1)
                dve.wait_ge(bn_done, n + 1)
                nc.vector.scalar_tensor_tensor(minus_twice[:, h], bn[:, h, :, 1], -1.0, bn[:, h, :, 4],
                                               ALU.mult, ALU.subtract).then_inc(twice_ready, 1)
                for u in range(2):
                    last = nc.vector.bn_aggr(mean_var[:, h, u], bn[:, h, u])
                last.then_inc(aggregated, 1)
                dve.wait_ge(aggregated, n + 1)
                nc.vector.tensor_scalar(var_eps[:, h], mean_var[:, h, :, 1], EPS, None, ALU.add).then_inc(spread_ready, 1)
                dve.wait_ge(twice_ready, n + 1)
                nc.vector.tensor_scalar(minus_mean[:, h], minus_twice[:, h], 0.5, None, ALU.mult).then_inc(spread_ready, 1)

            def norm_lo(s, name):
                dve.wait_ge(turned_hi, s.before("turn", name) + 1)
                nc.vector.tensor_tensor(turned_x(xt_lo, name), turn_ps[:].rearrange("p (c t) -> p c t", c=DC),
                                        turned_x(xt_hi, name).bitcast(F32), ALU.subtract).then_inc(turned_lo, 1)

            def silu(s, slot):
                n = s.before("chunk", slot)
                dve.wait_ge(tanh_ready, n + 1)
                nc.vector.scalar_tensor_tensor(gated[:, slot % 2], gated[:, slot % 2], 1.0, gate_ps[slot % 2][:],
                                               ALU.add, ALU.mult).then_inc(silu_ready, 1)

            def hidden(s, slot):
                n = s.before("chunk", slot)
                dve.wait_ge(silu_ready, n + 1)
                dve.wait_ge(up_ready, n + 1)
                reuse(dve, hid_lo_ready, n - 2)
                nc.vector.tensor_tensor(hid[:, slot % 3], gated[:, slot % 2], up_ps[slot % 2][:],
                                        ALU.mult).then_inc(hid_ready, 1)

            def rope_products(s, w):
                cos, sin = rope_sb[:, 0], rope_sb[:, 1]
                for c, products in enumerate((((cos, turned_qk[:, w, 0]), (sin, turned_qk[:, w, 1])),
                                              ((sin, cross[:, 0]), (cos, cross[:, 1])))):
                    dve.wait_ge(qk_ready, s.times(ATTEND, 4, 2 * w + c + 1))
                    if w == K and c == 1:
                        dve.wait_ge(rotated, s.times(ATTEND, 2, 1))
                    for table, product in products:
                        last = nc.vector.scalar_tensor_tensor(product, att_ps[c][:], qk_bias[:, w, c:c + 1], table,
                                                              ALU.add, ALU.mult)
                    last.then_inc(qk_taken, 1)

            def key_lo(s):
                dve.wait_ge(qk_hi_ready, s.times(ATTEND, 2, 2))
                nc.vector.tensor_tensor(qk_lo[:, K], turned_qk[:, K], qk_hi[:, K].bitcast(F32),
                                        ALU.subtract).then_inc(k_lo_ready, 1)

            def values_lo(s, pair):
                dve.wait_ge(v_hi_ready, s.times(ATTEND, 2, pair + 1))
                nc.vector.tensor_tensor(v_lo[:, 2 * pair:2 * pair + 2], att_ps[pair][:].rearrange("p (u d) -> p u d", u=2),
                                        v_hi[:, 2 * pair:2 * pair + 2].bitcast(F32), ALU.subtract).then_inc(v_lo_ready, 1)

            def row_max(s, t):
                dve.wait_ge(score_ready, s.times(ATTEND, TILES, t + 1))
                nc.vector.tensor_reduce(minus_max[:, t:t + 1], att_ps[t % 2][:], AX_X, ALU.max,
                                        negate=True).then_inc(max_ready, 1)
                dve.wait_ge(max_ready, s.times(ATTEND, TILES, t + 1))
                nc.vector.tensor_scalar(exp_bias[:, t:t + 1], minus_max[:, t:t + 1], D ** -0.5, None,
                                        ALU.mult).then_inc(bias_ready, 1)

            def prob_lo(s, t):
                dve.wait_ge(turned_hi, s.before("turn", f"p{t}") + 1)
                nc.vector.tensor_tensor(pt_lo[:], turn_ps[:].rearrange("p (k q) -> p k q", k=TILES),
                                        pt_hi[:].bitcast(F32), ALU.subtract).then_inc(turned_lo, 1)
                nc.vector.reciprocal(prob_inv[:, t:t + 1], prob_sum[:, t:t + 1]).then_inc(inv_ready, 1)

            def attended(s, t):
                dve.wait_ge(out_ready, s.before("out", f"attend{t}") + 1)
                dve.wait_ge(inv_ready, s.times(ATTEND, TILES, t + 1))
                if t == 0:
                    dve.wait_ge(v_bias_added, s.times(ATTEND, 1, 1))
                    reuse(dve, x_second_copied, s.times(ATTEND, 16, 0))
                nc.vector.scalar_tensor_tensor(x_norm3[:, t], out_ps[:, 0:D], prob_inv[:, t:t + 1], x_attend[:, t],
                                               ALU.mult, ALU.add).then_inc(out_taken, 1)

            def fed(s, stage, t, name, source, target):
                dve.wait_ge(out_ready, s.before("out", f"{name}{t}") + 1)
                if t == 0 and stage == FIRST:
                    dve.wait_ge(x_first_copied, s.times(FIRST, 16, 16))
                if t == 0 and stage == SECOND_DOWN:
                    dve.wait_ge(x_second_copied, s.times(SECOND_DOWN, 16, 16))
                nc.vector.scalar_tensor_tensor(target[:, t], down_bank(s, t)[:, 0:D], 0.25 * WEIGHT_SCALE ** 3, source[:, t],
                                               ALU.mult, ALU.add).then_inc(out_taken, 1)

            def iteration(s):
                attend = s.has(ATTEND)
                for slot in range(SLOTS):
                    for name in s.norms(slot, STATISTICS):
                        if name in EARLY:
                            statistics(s, name)
                    if attend and 8 <= slot < 8 + TILES:
                        attended(s, slot - 8)
                    if s.has(chunk_stage(slot)):
                        silu(s, slot)
                    for name in s.norms(slot, TURN):
                        norm_lo(s, name)
                    if s.has(FIRST) and 7 <= slot < 7 + TILES:
                        fed(s, FIRST, slot - 7, "first", x_first, x_first)
                    if s.has(chunk_stage(slot)):
                        hidden(s, slot)
                    if s.has(SECOND_DOWN) and 1 <= slot < 1 + TILES:
                        fed(s, SECOND_DOWN, slot - 1, "second", x_second, x_second)
                    if attend and 7 <= slot < 7 + TILES:
                        prob_lo(s, slot - 7)
                    if attend and slot == 1:
                        rope_products(s, Q)
                    if attend and slot == 4:
                        key_lo(s)
                    if attend and slot == 2:
                        rope_products(s, K)
                    if attend and 6 <= slot < 6 + TILES:
                        row_max(s, slot - 6)
                    for name in s.norms(slot, STATISTICS):
                        if name not in EARLY:
                            statistics(s, name)
                    if attend and slot == 4:
                        values_lo(s, 0)
                        values_lo(s, 1)

            def cast_weight(n):
                dve.wait_ge(w_loaded[n], 16)
                nc.vector.tensor_copy(raw[n], raw[n].bitcast(I32)).then_inc(cast, 1)

            def weight_lo(g):
                dve.wait_ge(setup_hi, g + 1)
                nc.vector.tensor_tensor(groups[g][3], setup_ps[g % len(setup_ps)][:], groups[g][2].bitcast(F32),
                                        ALU.subtract).then_inc(setup_lo, 1)

            cast_weight(GATE)
            cast_weight(UP)
            statistics(first, "n1a")
            statistics(first, "n1b")
            for g in range(FFN_GROUPS):
                weight_lo(g)
            cast_weight(DOWN)
            for g in range(FFN_GROUPS, 2 * FFN_GROUPS):
                weight_lo(g)
            norm_lo(first, "n1a")
            for g in range(2 * FFN_GROUPS, 3 * FFN_GROUPS):
                weight_lo(g)
            norm_lo(first, "n1b")
            dve.wait_ge(squared, 3)
            nc.vector.tensor_reduce(lo_total[:], lo_squares[:], AX_X, ALU.add).then_inc(total_ready, 1)
            dve.wait_ge(total_copied, 1)
            nc.vector.tensor_scalar(wide_flag[:], turn_ps[0:1, 0:1], 1.0, None, ALU.min).then_inc(flag_ready, 1)
            for g in range(3 * FFN_GROUPS, GROUPS):
                weight_lo(g)
            dve.wait_ge(const_loaded, 16 * 4)

            run(dve, iteration)

        @block.tensor
        def _(pe):
            def norm_turn(s, name):
                h = half[name[2]]
                norms_done = s.start("norm") if name == "n2b" else s.after("norm", name)
                reuse(pe, turned_lo, s.before("turn", name))
                for u in range(2):
                    pe.wait_ge((first_tile_normed, normed)[u], norms_done)
                    for c in range(DC):
                        last = nc.tensor.transpose(turn_ps[:, c * 2 * P + u * P:c * 2 * P + (u + 1) * P],
                                                   xn[:, h, u, c * P:(c + 1) * P], ident[:])
                last.then_inc(turned, 1)

            pe.wait_ge(made, 4)
            for g, (weight, blocks, _, _) in enumerate(groups):
                if weight < 3:
                    pe.wait_ge(cast, weight + 1)
                else:
                    pe.wait_ge(w_loaded[weight], 16)
                reuse(pe, setup_lo, g - len(setup_ps) + 1)
                for n, b in enumerate(blocks):
                    last = nc.tensor.transpose(setup_ps[g % len(setup_ps)][:, n * P:(n + 1) * P], b, ident[:])
                last.then_inc(setup_turned, 1)
                if g == 2 * FFN_GROUPS - 1:
                    norm_turn(first, "n1a")
                if g == 3 * FFN_GROUPS - 1:
                    norm_turn(first, "n1b")
            pe.wait_ge(total_ready, 1)
            nc.tensor.matmul(turn_ps[0:1, 0:1], lo_total[:], ones[:, 0:1], start=True, stop=True).then_inc(total_copied, 1)
            pe.wait_ge(flag_ready, 1)
            wide = pe.value_load(wide_flag[0:1, 0:1], min_val=0, max_val=1)

            def products(out, terms, first=True, last=True):
                for n, (lhs_t, rhs) in enumerate(terms):
                    product = nc.tensor.matmul(out, lhs_t, rhs, start=(first and n == 0), stop=(last and n == len(terms) - 1))
                return product

            def program(ffn_passes):
                def chunk(s, slot, w, ps, ready):
                    n = s.before("chunk", slot)
                    h = slot % CHUNKS
                    norm = 1 if slot < CHUNKS else 3
                    first_use = w == GATE and h == 0
                    turns = s.start("turn") if norm == 1 else s.after("turn", "n3b")
                    if first_use:
                        pe.wait_ge(turned_hi, turns)
                    reuse(pe, silu_ready if w == GATE else hid_ready, n - 1)
                    with_hi, with_lo = [], []
                    for c in range(DC):
                        hi, lo = (part[:, w, c * HIDDEN + h * P:c * HIDDEN + (h + 1) * P] for part in (ffn_hi, ffn_lo))
                        with_hi += [(hi, xt_hi[norm][:, c]), (lo, xt_hi[norm][:, c])][:ffn_passes - 1]
                        with_lo += [(hi, xt_lo[norm][:, c])]
                    products(ps[slot % 2][:], with_hi, last=False)
                    if first_use:
                        pe.wait_ge(turned_lo, turns)
                    products(ps[slot % 2][:], with_lo, first=False).then_inc(ready, 1)

                def down(s, f, name, t, chunks_done):
                    if s.i == START + 1:
                        pe.wait_ge(setup_lo, GROUPS)
                    reuse(pe, out_taken, s.before("out", f"{name}{t}") - (s.i == END - 1 and t > 0))
                    for h in range(CHUNKS):
                        hi, lo = (part[f][:, h, t * P:(t + 1) * P] for part in (hid_hi, hid_lo))
                        w_hi, w_lo = (part[:, DOWN, h * D:(h + 1) * D] for part in (ffn_hi, ffn_lo))
                        if t == 0:
                            pe.wait_ge(hid_lo_ready, chunks_done - CHUNKS + 1 + h)
                        terms = [(hi, w_hi), (lo, w_hi), (hi, w_lo)][:ffn_passes]
                        last = products(down_bank(s, t)[:, 0:D], terms, h == 0, h == CHUNKS - 1)
                    last.then_inc(out_ready, 1)

                def project(s, w):
                    if w == Q:
                        pe.wait_ge(turned_hi, s.after("turn", "n2b"))
                        reuse(pe, exp_ready, s.times(ATTEND, TILES, 0))
                    for c in range(DC):
                        with_hi, with_lo = [], []
                        for dc in range(DC):
                            hi, lo = (part[:, w, (dc * DC + c) * P:(dc * DC + c + 1) * P] for part in (qkv_hi, qkv_lo))
                            with_hi += [(hi, xt_hi[2][:, dc]), (lo, xt_hi[2][:, dc])]
                            with_lo += [(hi, xt_lo[2][:, dc])]
                        if w == K:
                            pe.wait_ge(qk_taken, s.times(ATTEND, 4, c + 1))
                        products(att_ps[c][:], with_hi, last=False)
                        if w == Q and c == 0:
                            pe.wait_ge(turned_lo, s.after("turn", "n2b"))
                        products(att_ps[c][:], with_lo, first=False).then_inc(qk_ready, 1)

                def values(s, pair):
                    pe.wait_ge(qk_taken, s.times(ATTEND, 4, 2 + pair + 1))
                    for u in range(2):
                        at = (2 * pair + u) * P
                        terms = []
                        for dc in range(DC):
                            hi, lo = (part[:, V, dc * D:(dc + 1) * D] for part in (qkv_hi, qkv_lo))
                            x_hi, x_lo = xt_hi[2][:, dc, at:at + P], xt_lo[2][:, dc, at:at + P]
                            terms += [(x_hi, hi), (x_hi, lo), (x_lo, hi)]
                        last = products(att_ps[pair][:, u * D:(u + 1) * D], terms)
                    last.then_inc(v_ready, 1)

                def scores(s, t):
                    if t == 0:
                        pe.wait_ge(qk_hi_ready, s.times(ATTEND, 2, 2))
                    if t < 2:
                        pe.wait_ge(v_lo_ready, s.times(ATTEND, 2, t + 1))
                    else:
                        pe.wait_ge(exp_ready, s.times(ATTEND, TILES, t - 1))
                    q_hi, q_lo = (part[:, Q, :, t * P:(t + 1) * P] for part in (qk_hi, qk_lo))
                    products(att_ps[t % 2][:], [(q_hi[:, c], qk_hi[:, K, c]) for c in range(DC)], last=False)
                    if t == 0:
                        pe.wait_ge(q_lo_ready, s.times(ATTEND, 1, 1))
                    products(att_ps[t % 2][:], [(q_lo[:, c], qk_hi[:, K, c]) for c in range(DC)], first=False, last=False)
                    if t == 0:
                        pe.wait_ge(k_lo_ready, s.times(ATTEND, 1, 1))
                    products(att_ps[t % 2][:], [(q_hi[:, c], qk_lo[:, K, c]) for c in range(DC)],
                             first=False).then_inc(score_ready, 1)

                def prob_turn(s, t):
                    pe.wait_ge(exp_ready, s.times(ATTEND, TILES, t + 1))
                    reuse(pe, turned_lo, s.before("turn", f"p{t}"))
                    for k in range(TILES):
                        last = nc.tensor.transpose(turn_ps[:, k * P:(k + 1) * P], prob[:, t % 2, k * P:(k + 1) * P], ident[:])
                    last.then_inc(turned, 1)

                def weigh(s, t):
                    pe.wait_ge(turned_hi, s.after("turn", f"p{t}"))
                    reuse(pe, out_taken, s.before("out", f"attend{t}"))
                    products(out_ps[:, 0:D], [(pt_hi[:, k], v[:, k]) for k in range(TILES) for v in (v_hi, v_lo)], last=False)
                    pe.wait_ge(turned_lo, s.after("turn", f"p{t}"))
                    products(out_ps[:, 0:D], [(pt_lo[:, k], v_hi[:, k]) for k in range(TILES)],
                             first=False).then_inc(out_ready, 1)

                def iteration(s):
                    attend = s.has(ATTEND)
                    for slot in range(SLOTS):
                        if s.has(chunk_stage(slot)):
                            chunk(s, slot, GATE, gate_ps, gate_ready)
                        if attend and 8 <= slot < 8 + TILES:
                            weigh(s, slot - 8)
                        if s.has(chunk_stage(slot)):
                            chunk(s, slot, UP, up_ps, up_ready)
                        for name in s.norms(slot, TURN):
                            norm_turn(s, name)
                        if s.has(SECOND_DOWN) and 1 <= slot < 1 + TILES:
                            down(s, SECOND, "second", slot - 1, s.start("chunk"))
                        if attend and slot == 4:
                            values(s, 0)
                            values(s, 1)
                        if s.has(FIRST) and 7 <= slot < 7 + TILES:
                            down(s, FIRST, "first", slot - 7, s.after("chunk", CHUNKS - 1))
                        if attend and 7 <= slot < 7 + TILES:
                            prob_turn(s, slot - 7)
                        if attend and 6 <= slot < 6 + TILES:
                            scores(s, slot - 6)
                        if attend and slot == 1:
                            project(s, Q)
                        if attend and slot == 2:
                            project(s, K)

                run(pe, iteration)

            with pe.If(wide > 0):
                program(3)
            with pe.Else():
                program(2)


def rope_tables():
    inv_freq = (1.0 / np.float32(THETA) ** (np.arange(0, D, 2, dtype=np.float32) / np.float32(D))).astype(np.float32)
    token = np.arange(TOKENS).reshape(P, TILES).T.reshape(-1).astype(np.float32)
    angle = inv_freq[:, None] * token[None, :]
    return np.stack([np.cos(angle), np.sin(angle)]).astype(np.float32)


INPUTS = ["L0_attn_x", "L0_attn_wq_w", "L0_attn_wq_b", "L0_attn_wk_w", "L0_attn_wk_b", "L0_attn_wv_w",
          "L0_attn_wv_b", "L0_ffn_w_gate", "L0_ffn_w_up", "L0_ffn_w_down"]


def kernel(**inputs):
    import concourse.bacc as bacc
    from concourse.bass_utils import run_bass_kernel_spmd

    nc = bacc.Bacc("TRN2", target_bir_lowering=False, num_devices=1)
    arrays = {name: np.ascontiguousarray(inputs[name]) for name in INPUTS}
    arrays["rope"] = rope_tables()
    args = [nc.dram_tensor(f"in_{name}", a.shape, mybir.dt.from_np(a.dtype), kind="ExternalInput").ap()
            for name, a in arrays.items()]
    out = nc.dram_tensor("out", (BATCHES, TOKENS, D), F32, kind="ExternalOutput").ap()
    build(nc, *args, out)
    result = run_bass_kernel_spmd(nc, [{f"in_{name}": a for name, a in arrays.items()}], core_ids=[0])
    return result.results[0]["out"]
```
